# Optimizing a Trainium2 kernel written in Bass

```python
import numpy as np
import jax
import jax.numpy as jnp

def _softmax(x, axis=-1):
    return jax.nn.softmax(x, axis=axis)

def _gelu(x):
    return jax.nn.gelu(x, approximate=True)

def _silu(x):
    return jax.nn.silu(x)

def _sigmoid(x):
    return jax.nn.sigmoid(x)

def _layernorm(x, axis=-1, eps=1e-05):
    m = jnp.mean(x, axis=axis, keepdims=True)
    v = jnp.var(x, axis=axis, keepdims=True)
    return (x - m) / jnp.sqrt(v + eps)

def _scatter_add(tgt, idx, src, axis=0):
    return tgt.at[idx].add(src)

def _segment_sum(src, seg, n):
    return jax.ops.segment_sum(src, seg, n)
kernel_name = 'mk_macaron_d1_jaxref_r8_f04208'

def setup_inputs(seed: int=0):
    np.random.seed(seed)
    _w = jnp.asarray

    def _L0_attn_setup():
        import jax, jax.numpy as jnp
        import numpy as np
        BLOCK = 32
        NUM_HEADS = 16
        HEAD_DIM = 128
        FP4_GRID = jnp.array([0.0, 0.5, 1.0, 1.5, 2.0, 3.0, 4.0, 6.0], dtype=jnp.float32)

        def quantize_to_mxfp4(w, block_size=BLOCK):
            D, F = w.shape
            blocks = w.reshape(D // block_size, block_size, F)
            amax = jnp.max(jnp.abs(blocks), axis=1)
            e = jnp.floor(jnp.log2(jnp.maximum(amax, 1e-12) / 6.0))
            scale = jnp.exp2(e)
            v = blocks / scale[:, None, :]
            idx = jnp.argmin(jnp.abs(jnp.abs(v)[..., None] - FP4_GRID), axis=-1)
            codes = jnp.sign(v) * FP4_GRID[idx]
            return (codes.reshape(D, F).astype(jnp.float32), scale.astype(jnp.float32))

        def _mxfp4_matmul(x, codes, scales, block_size=BLOCK):
            w = codes * jnp.repeat(scales, block_size, axis=0)
            return x @ w
        key = jax.random.key(seed)
        ks = jax.random.split(key, 9)
        B, S, D = (2, 256, 256)
        feat = NUM_HEADS * HEAD_DIM
        x = jax.random.normal(ks[0], (B, S, D), dtype=jnp.float32)

        def make_w(k, din, dout):
            w = jax.random.normal(k, (din, dout), dtype=jnp.float32) * (1.0 / np.sqrt(din))
            return quantize_to_mxfp4(w, BLOCK)
        wq_codes, wq_scales = make_w(ks[1], D, feat)
        wk_codes, wk_scales = make_w(ks[2], D, feat)
        wv_codes, wv_scales = make_w(ks[3], D, feat)
        wo_codes, wo_scales = make_w(ks[4], feat, D)
        bq = jnp.zeros((feat,), jnp.float32)
        bk = jnp.zeros((feat,), jnp.float32)
        bv = jnp.zeros((feat,), jnp.float32)
        bo = jnp.zeros((D,), jnp.float32)
        return {'x': x, 'wq_codes': wq_codes, 'wq_scales': wq_scales, 'bq': bq, 'wk_codes': wk_codes, 'wk_scales': wk_scales, 'bk': bk, 'wv_codes': wv_codes, 'wv_scales': wv_scales, 'bv': bv, 'wo_codes': wo_codes, 'wo_scales': wo_scales, 'bo': bo}
    _L0_attn_in = _L0_attn_setup()

    def _L0_ffn_setup():
        import jax, jax.numpy as jnp
        import numpy as np
        B, T, D = (1, 256, 256)
        E, K, F = (64, 4, 64)
        S, SF = (2, 64 * 4)
        CAP = 32

        def _moe_forward(x, router_w, router_bias, gate_w, up_w, down_w, sh_gate_w, sh_up_w, sh_down_w):
            b, t, d = x.shape
            flat = x.reshape(b * t, d)
            N = flat.shape[0]
            logits = flat @ router_w.T
            scores = jax.nn.softmax(logits, axis=-1)
            _, topk_idx = jax.lax.top_k(logits + router_bias, K)
            topk_w = jnp.take_along_axis(scores, topk_idx, axis=-1)
            topk_w = topk_w / topk_w.sum(axis=-1, keepdims=True)
            P = N * K
            e_flat = topk_idx.reshape(-1)
            t_flat = jnp.repeat(jnp.arange(N), K)
            w_flat = topk_w.reshape(-1)
            order = jnp.argsort(e_flat)
            e_s, t_s, w_s = (e_flat[order], t_flat[order], w_flat[order])
            counts = jnp.bincount(e_s, length=E)
            starts = jnp.concatenate([jnp.zeros((1,), counts.dtype), jnp.cumsum(counts)[:-1]])
            pos = jnp.arange(P) - starts[e_s]
            slot = jnp.where(pos < CAP, pos, CAP)
            tok_table = jnp.zeros((E, CAP + 1), jnp.int32).at[e_s, slot].set(t_s)[:, :CAP]
            w_table = jnp.zeros((E, CAP + 1), w_s.dtype).at[e_s, slot].set(w_s)[:, :CAP]
            xg = flat[tok_table]
            g = jnp.einsum('ecd,efd->ecf', xg, gate_w)
            u = jnp.einsum('ecd,efd->ecf', xg, up_w)
            y = jnp.einsum('ecf,edf->ecd', jax.nn.silu(g) * u, down_w)
            out = jnp.zeros_like(flat).at[tok_table.reshape(-1)].add((y * w_table[..., None]).reshape(-1, d))
            sg = jnp.einsum('nd,sfd->nsf', flat, sh_gate_w)
            su = jnp.einsum('nd,sfd->nsf', flat, sh_up_w)
            out = out + jnp.einsum('nsf,sdf->nd', jax.nn.silu(sg) * su, sh_down_w)
            return out.reshape(b, t, d)
        key = jax.random.key(seed)
        ks = jax.random.split(key, 9)
        s = 0.02
        return {'x': jax.random.normal(ks[0], (B, T, D), jnp.float32), 'router_w': jax.random.normal(ks[1], (E, D), jnp.float32) * s, 'router_bias': jnp.zeros((E,), jnp.float32), 'gate_w': jax.random.normal(ks[2], (E, F, D), jnp.float32) * s, 'up_w': jax.random.normal(ks[3], (E, F, D), jnp.float32) * s, 'down_w': jax.random.normal(ks[4], (E, D, F), jnp.float32) * s, 'sh_gate_w': jax.random.normal(ks[5], (S, SF, D), jnp.float32) * s, 'sh_up_w': jax.random.normal(ks[6], (S, SF, D), jnp.float32) * s, 'sh_down_w': jax.random.normal(ks[7], (S, D, SF), jnp.float32) * s}
    _L0_ffn_in = _L0_ffn_setup()
    _d = {'L0_attn_x': _L0_attn_in['x'], 'L0_attn_wq_codes': _L0_attn_in['wq_codes'], 'L0_attn_wq_scales': _L0_attn_in['wq_scales'], 'L0_attn_bq': _L0_attn_in['bq'], 'L0_attn_wk_codes': _L0_attn_in['wk_codes'], 'L0_attn_wk_scales': _L0_attn_in['wk_scales'], 'L0_attn_bk': _L0_attn_in['bk'], 'L0_attn_wv_codes': _L0_attn_in['wv_codes'], 'L0_attn_wv_scales': _L0_attn_in['wv_scales'], 'L0_attn_bv': _L0_attn_in['bv'], 'L0_attn_wo_codes': _L0_attn_in['wo_codes'], 'L0_attn_wo_scales': _L0_attn_in['wo_scales'], 'L0_attn_bo': _L0_attn_in['bo'], 'L0_ffn_router_w': _L0_ffn_in['router_w'], 'L0_ffn_router_bias': _L0_ffn_in['router_bias'], 'L0_ffn_gate_w': _L0_ffn_in['gate_w'], 'L0_ffn_up_w': _L0_ffn_in['up_w'], 'L0_ffn_down_w': _L0_ffn_in['down_w'], 'L0_ffn_sh_gate_w': _L0_ffn_in['sh_gate_w'], 'L0_ffn_sh_up_w': _L0_ffn_in['sh_up_w'], 'L0_ffn_sh_down_w': _L0_ffn_in['sh_down_w']}
    _x0 = _d['L0_attn_x']
    _d['L0_attn_x'] = jax.random.normal(jax.random.fold_in(jax.random.key(seed), 1), (4, 512, 256), dtype=_x0.dtype)
    del _x0
    return _d

def reference(L0_attn_x, L0_attn_wq_codes, L0_attn_wq_scales, L0_attn_bq, L0_attn_wk_codes, L0_attn_wk_scales, L0_attn_bk, L0_attn_wv_codes, L0_attn_wv_scales, L0_attn_bv, L0_attn_wo_codes, L0_attn_wo_scales, L0_attn_bo, L0_ffn_router_w, L0_ffn_router_bias, L0_ffn_gate_w, L0_ffn_up_w, L0_ffn_down_w, L0_ffn_sh_gate_w, L0_ffn_sh_up_w, L0_ffn_sh_down_w):

    def _L0_attn_ref(x, wq_codes, wq_scales, bq, wk_codes, wk_scales, bk, wv_codes, wv_scales, bv, wo_codes, wo_scales, bo):
        import jax, jax.numpy as jnp
        import numpy as np
        BLOCK = 32
        NUM_HEADS = 16
        HEAD_DIM = 128
        FP4_GRID = jnp.array([0.0, 0.5, 1.0, 1.5, 2.0, 3.0, 4.0, 6.0], dtype=jnp.float32)

        def quantize_to_mxfp4(w, block_size=BLOCK):
            D, F = w.shape
            blocks = w.reshape(D // block_size, block_size, F)
            amax = jnp.max(jnp.abs(blocks), axis=1)
            e = jnp.floor(jnp.log2(jnp.maximum(amax, 1e-12) / 6.0))
            scale = jnp.exp2(e)
            v = blocks / scale[:, None, :]
            idx = jnp.argmin(jnp.abs(jnp.abs(v)[..., None] - FP4_GRID), axis=-1)
            codes = jnp.sign(v) * FP4_GRID[idx]
            return (codes.reshape(D, F).astype(jnp.float32), scale.astype(jnp.float32))

        def _mxfp4_matmul(x, codes, scales, block_size=BLOCK):
            w = codes * jnp.repeat(scales, block_size, axis=0)
            return x @ w
        B, S, D = x.shape
        q = _mxfp4_matmul(x, wq_codes, wq_scales) + bq
        k = _mxfp4_matmul(x, wk_codes, wk_scales) + bk
        v = _mxfp4_matmul(x, wv_codes, wv_scales) + bv
        q = q.reshape(B, S, NUM_HEADS, HEAD_DIM)
        k = k.reshape(B, S, NUM_HEADS, HEAD_DIM)
        v = v.reshape(B, S, NUM_HEADS, HEAD_DIM)
        scores = jnp.einsum('bqhd,bkhd->bhqk', q, k) / jnp.sqrt(jnp.float32(HEAD_DIM))
        attn = jax.nn.softmax(scores, axis=-1)
        out = jnp.einsum('bhqk,bkhd->bqhd', attn, v).reshape(B, S, NUM_HEADS * HEAD_DIM)
        return _mxfp4_matmul(out, wo_codes, wo_scales) + bo

    def _L0_ffn_ref(x, router_w, router_bias, gate_w, up_w, down_w, sh_gate_w, sh_up_w, sh_down_w):
        import jax, jax.numpy as jnp
        import numpy as np
        B, T, D = (1, 256, 256)
        E, K, F = (64, 4, 64)
        S, SF = (2, 64 * 4)
        CAP = 32

        def _moe_forward(x, router_w, router_bias, gate_w, up_w, down_w, sh_gate_w, sh_up_w, sh_down_w):
            b, t, d = x.shape
            flat = x.reshape(b * t, d)
            N = flat.shape[0]
            logits = flat @ router_w.T
            scores = jax.nn.softmax(logits, axis=-1)
            _, topk_idx = jax.lax.top_k(logits + router_bias, K)
            topk_w = jnp.take_along_axis(scores, topk_idx, axis=-1)
            topk_w = topk_w / topk_w.sum(axis=-1, keepdims=True)
            P = N * K
            e_flat = topk_idx.reshape(-1)
            t_flat = jnp.repeat(jnp.arange(N), K)
            w_flat = topk_w.reshape(-1)
            order = jnp.argsort(e_flat)
            e_s, t_s, w_s = (e_flat[order], t_flat[order], w_flat[order])
            counts = jnp.bincount(e_s, length=E)
            starts = jnp.concatenate([jnp.zeros((1,), counts.dtype), jnp.cumsum(counts)[:-1]])
            pos = jnp.arange(P) - starts[e_s]
            slot = jnp.where(pos < CAP, pos, CAP)
            tok_table = jnp.zeros((E, CAP + 1), jnp.int32).at[e_s, slot].set(t_s)[:, :CAP]
            w_table = jnp.zeros((E, CAP + 1), w_s.dtype).at[e_s, slot].set(w_s)[:, :CAP]
            xg = flat[tok_table]
            g = jnp.einsum('ecd,efd->ecf', xg, gate_w)
            u = jnp.einsum('ecd,efd->ecf', xg, up_w)
            y = jnp.einsum('ecf,edf->ecd', jax.nn.silu(g) * u, down_w)
            out = jnp.zeros_like(flat).at[tok_table.reshape(-1)].add((y * w_table[..., None]).reshape(-1, d))
            sg = jnp.einsum('nd,sfd->nsf', flat, sh_gate_w)
            su = jnp.einsum('nd,sfd->nsf', flat, sh_up_w)
            out = out + jnp.einsum('nsf,sdf->nd', jax.nn.silu(sg) * su, sh_down_w)
            return out.reshape(b, t, d)
        return _moe_forward(x, router_w, router_bias, gate_w, up_w, down_w, sh_gate_w, sh_up_w, sh_down_w)
    x = L0_attn_x
    x = x + 0.5 * _L0_ffn_ref(_layernorm(x, axis=-1), L0_ffn_router_w, L0_ffn_router_bias, L0_ffn_gate_w, L0_ffn_up_w, L0_ffn_down_w, L0_ffn_sh_gate_w, L0_ffn_sh_up_w, L0_ffn_sh_down_w)
    x = x + _L0_attn_ref(_layernorm(x, axis=-1), L0_attn_wq_codes, L0_attn_wq_scales, L0_attn_bq, L0_attn_wk_codes, L0_attn_wk_scales, L0_attn_bk, L0_attn_wv_codes, L0_attn_wv_scales, L0_attn_bv, L0_attn_wo_codes, L0_attn_wo_scales, L0_attn_bo)
    x = x + 0.5 * _L0_ffn_ref(_layernorm(x, axis=-1), L0_ffn_router_w, L0_ffn_router_bias, L0_ffn_gate_w, L0_ffn_up_w, L0_ffn_down_w, L0_ffn_sh_gate_w, L0_ffn_sh_up_w, L0_ffn_sh_down_w)
    return x

_drawn_inputs = setup_inputs


def setup_inputs(seed=0):
    import zlib

    import numpy as np

    out = dict(_drawn_inputs(seed))
    spreads = {'L0_attn_bq': (0.0, 0.8),
     'L0_attn_bk': (0.0, 0.8),
     'L0_attn_bv': (0.0, 0.1),
     'L0_attn_bo': (0.0, 0.1),
     'L0_ffn_router_bias': (0.0, 0.8)}
    factors = {'L0_attn_wq_scales': 4.061,
     'L0_attn_wk_scales': 4.068,
     'L0_attn_wv_scales': 3.759,
     'L0_ffn_router_w': 8.0,
     'L0_ffn_gate_w': 8.0,
     'L0_ffn_up_w': 8.0,
     'L0_ffn_down_w': 8.0}
    for name, (base, spread) in spreads.items():
        noise = np.random.default_rng([zlib.crc32(name.encode()), seed]).standard_normal(out[name].shape)
        drawn = base * np.exp(spread * noise) if base else spread * noise
        out[name] = jnp.asarray(drawn.astype(out[name].dtype))
    for name, factor in factors.items():
        out[name] = (out[name] * factor).astype(out[name].dtype)
    return out
```

```python
from contextlib import ExitStack

import numpy as np
import concourse.bass as bass
from concourse import mybir

F32 = mybir.dt.float32
F32R = mybir.dt.float32r
I32 = mybir.dt.int32
U32 = mybir.dt.uint32
BF16 = mybir.dt.bfloat16
ACT = mybir.ActivationFunctionType
ALU = mybir.AluOpType
X = mybir.AxisListType.X

P = 128
D = 256
DC = D // P
N = 2048
NT = N // P
E = 64
K = 4
F = 64
CAP = 32
SH = 512
SM = SH // P
EPS = 1e-5
CH = 512
NCH = N // CH
EG = 4
NG = E // EG
ROW = D + E
H = 16
B = 4
S = 512
HD = 128
FEAT = H * HD
BLK = 32
SCALE = 1.0 / float(np.sqrt(np.float32(HD)))


ROUTE_STEPS = 3 + 2 + 2 + 2 * (K - 1) + 7


def f32(ap):
    return ap.bitcast(F32)


def apart(eng, passed):
    eng.sem_inc(passed, 1)


class Counter:

    def __init__(self, eng, sem, base):
        self.eng, self.sem, self.base, self.n = eng, sem, base, 0

    def then(self, ins, passed=None):
        self.n += 1
        ins.then_inc(self.sem, 1)
        self.eng.wait_ge(self.sem, self.base + self.n)
        if passed is not None:
            apart(self.eng, passed)


class Memory:
    def __init__(self, nc, ctx, tag):
        self.nc, self.ctx, self.tag, self.sems = nc, ctx, tag, []

    def sb(self, name, shape, dt=F32):
        return self.ctx.enter_context(self.nc.sbuf_tensor(f"{self.tag}_{name}", shape, dt))

    def ps(self, name, shape=(P, 512), dt=F32):
        return self.ctx.enter_context(self.nc.psum_tensor(f"{self.tag}_{name}", list(shape), dt))

    def sem(self, name):
        if not self.sems:
            self.ctx.callback(self.clear)
        self.sems.append(self.nc.alloc_semaphore(name=f"{self.tag}_{name}"))
        return self.sems[-1]

    def clear(self):
        self.nc.clear_and_free_semaphores(self.sems)
        self.nc.all_engine_barrier()


def prepare(nc, m, a):
    c = dict(
        x=m.sb("x", [P, NT, D]), ident=m.sb("ident", [P, P]),
        iota_e=m.sb("iota_e", [P, E]), iota_t=m.sb("iota_t", [P, N]), down_t=m.sb("down_t", [E, N]),
        sel=m.sb("sel", [P, 124]), mhalf=m.sb("mhalf", [P, NT]),
        rbias=m.sb("rbias", [P, E]), bo=m.sb("bo", [P, D]),
        bq=m.sb("bq", [P, H]), bk=m.sb("bk", [P, H]), bv=m.sb("bv", [P, H]),
        rw=[m.sb(f"rw{k}", [P, DC, P], F32R) for k in range(2)],
        gw=[m.sb(f"gw{k}", [P, DC, SH], F32R) for k in range(2)],
        uw=[m.sb(f"uw{k}", [P, DC, SH], F32R) for k in range(2)],
        dw=[m.sb(f"dw{k}", [P, SM, D], F32R) for k in range(2)],
    )
    with ExitStack() as ctx:
        t = Memory(nc, ctx, "prep")
        raw_g = t.sb("raw_g", [P, SM, D])
        raw_u = t.sb("raw_u", [P, SM, D])
        raw_d = t.sb("raw_d", [P, 2, DC, D])
        raw_r = t.sb("raw_r", [E, D])
        raw_b = t.sb("raw_b", [H, 3, HD])
        banks = [t.ps(f"bank{k}") for k in range(2)]
        loaded, x_loaded, consts, zeroed = (t.sem(n) for n in ("loaded", "x_loaded", "consts", "zeroed"))
        turned, hi_done, lo_done = t.sem("turned"), t.sem("hi_done"), t.sem("lo_done")
        block = ctx.enter_context(nc.Block())
        n_loads = 10

        @block.sync
        def _(sp):
            sp.dma_start(raw_g[:], a["sh_gate_w"].rearrange("s (m p) d -> p (s m) d", p=P)).then_inc(loaded, 16)
            sp.dma_start(raw_u[:], a["sh_up_w"].rearrange("s (m p) d -> p (s m) d", p=P)).then_inc(loaded, 16)
            for s in range(2):
                sp.dma_start(raw_d[:, s, :, :], a["sh_down_w"][s].rearrange("(c p) f -> p c f", p=P)).then_inc(loaded, 16)
            sp.dma_start(raw_r[:], a["router_w"]).then_inc(loaded, 16)
            for i, b in enumerate(("bq", "bk", "bv")):
                sp.dma_start(raw_b[:, i, :], a[b].rearrange("(h d) -> h d", d=HD)).then_inc(loaded, 16)
            sp.dma_start(c["rbias"][:], a["router_bias"].partition_broadcast(P)).then_inc(loaded, 16)
            sp.dma_start(c["bo"][:], a["bo"].partition_broadcast(P)).then_inc(loaded, 16)
            sp.dma_start(c["x"][:], a["x"].rearrange("b (i p) d -> p (b i) d", p=P)).then_inc(x_loaded, 16)
            sp.wait_ge(x_loaded, 16)

        @block.gpsimd
        def _(pool):
            pool.memset(c["ident"][:], 0.0).then_inc(consts, 1)
            pool.wait_ge(consts, 1)
            pool.affine_select(out=c["ident"][:], in_=c["ident"][:], compare_op=ALU.not_equal, fill=1.0,
                               base=0, pattern=[[-1, P]], channel_multiplier=1).then_inc(consts, 1)
            pool.iota(c["iota_e"][:], [[1, E]], base=0, channel_multiplier=0,
                      allow_small_or_imprecise_dtypes=True).then_inc(consts, 1)
            pool.iota(c["iota_t"][:], [[1, N]], base=0, channel_multiplier=0,
                      allow_small_or_imprecise_dtypes=True).then_inc(consts, 1)
            pool.iota(c["down_t"][:], [[-1, N]], base=N, channel_multiplier=0,
                      allow_small_or_imprecise_dtypes=True).then_inc(consts, 1)

        jobs = []
        for raw, dst in ((raw_g, "gw"), (raw_u, "uw")):
            for k in range(DC):
                jobs.append(([raw[:, i, k * P:(k + 1) * P] for i in range(SM)], [w[:, k, :] for w in c[dst]], P))
        for s in range(2):
            jobs.append(([raw_d[:, s, k, i * P:(i + 1) * P] for i in range(2) for k in range(DC)],
                         [w[:, 2 * s:2 * s + 2, :].rearrange("p a b -> p (a b)") for w in c["dw"]], P))
        jobs.append(([raw_r[:, k * P:(k + 1) * P] for k in range(DC)], None, E))
        jobs.append(([raw_b[:, i, :] for i in range(3)], None, H))

        @block.tensor
        def _(pe):
            pe.wait_ge(loaded, 16 * n_loads)
            pe.wait_ge(consts, 2)
            for n, (src, dst, w) in enumerate(jobs):
                if n >= 2:
                    pe.wait_ge(lo_done, n - 1)
                for i, s in enumerate(src):
                    last = pe.transpose(banks[n % 2][:, i * w:(i + 1) * w], s, c["ident"][0:w, 0:w])
                last.then_inc(turned, 1)

        @block.scalar
        def _(act):
            for n, (src, dst, w) in enumerate(jobs):
                act.wait_ge(turned, n + 1)
                bank = banks[n % 2]
                if dst is not None:
                    act.activation(dst[0], bank[:], ACT.Copy).then_inc(hi_done, 1)
                elif w == E:
                    v = bank[:, 0:DC * E].rearrange("p (k e) -> p k e", k=DC)
                    act.activation(c["rw"][0][:, :, 0:E], v, ACT.Copy).then_inc(hi_done, 1)
                else:
                    act.activation(c["bq"][:], bank[:, 0:H], ACT.Copy)
                    act.activation(c["bk"][:], bank[:, H:2 * H], ACT.Copy)
                    act.activation(c["bv"][:], bank[:, 2 * H:3 * H], ACT.Copy).then_inc(hi_done, 1)

        @block.vector
        def _(dve):
            for w in c["rw"]:
                dve.memset(f32(w[:, :, E:P]), 0.0)
            dve.memset(c["mhalf"][:], -0.5)
            dve.memset(c["sel"][:], 0.0).then_inc(zeroed, 1)
            dve.wait_ge(zeroed, 1)
            for q in range(EG):
                dve.memset(c["sel"][q * CAP:(q + 1) * CAP, 60 + q:61 + q], 1.0)
            for n, (src, dst, w) in enumerate(jobs):
                dve.wait_ge(hi_done, n + 1)
                bank = banks[n % 2]
                if dst is not None:
                    dve.tensor_tensor(dst[1], bank[:], f32(dst[0]), ALU.subtract).then_inc(lo_done, 1)
                elif w == E:
                    v = bank[:, 0:DC * E].rearrange("p (k e) -> p k e", k=DC)
                    dve.tensor_tensor(c["rw"][1][:, :, 0:E], v, f32(c["rw"][0][:, :, 0:E]),
                                      ALU.subtract).then_inc(lo_done, 1)
    return c


def norm_sems(m):
    names = "stats moments var_ready rstd_ready xn_ready turned hi_done lo_done rows_out0 rows_out1"
    return {n: m.sem(f"ln_{n}") for n in names.split()}


def norm_buffers(m):
    return dict(stats=m.sb("ln_stats", [P, NT, 6]), mean=m.sb("ln_mean", [P, NT]), var=m.sb("ln_var", [P, NT]),
                tmp=m.sb("ln_tmp", [P, NT]), rstd=m.sb("ln_rstd", [P, NT]),
                xn=[m.sb(f"ln_xn{s}", [P, 2, D]) for s in range(2)])


def norm_vector(dve, c, b, s, xT, rows):
    with dve.Fori(0, NT) as i:
        dve.bn_stats(b["stats"][:, bass.ds(i, 1), :], c["x"][:, bass.ds(i, 1), :]).then_inc(s["stats"], 1)
    dve.wait_ge(s["stats"], NT)
    st = b["stats"]
    mo = Counter(dve, s["moments"], 0)
    mo.then(dve.tensor_tensor(b["mean"][:], st[:, :, 1], st[:, :, 4], ALU.add))
    mo.then(dve.tensor_scalar(b["mean"][:], b["mean"][:], 0.5, None, ALU.mult))
    mo.then(dve.tensor_tensor(b["tmp"][:], st[:, :, 1], st[:, :, 4], ALU.subtract))
    mo.then(dve.scalar_tensor_tensor(out=b["tmp"][:], in0=b["tmp"][:], scalar=0.25, in1=b["tmp"][:],
                                     op0=ALU.mult, op1=ALU.mult))
    mo.then(dve.tensor_tensor(b["var"][:], st[:, :, 2], st[:, :, 5], ALU.add))
    mo.then(dve.scalar_tensor_tensor(out=b["var"][:], in0=b["var"][:], scalar=1.0 / D, in1=b["tmp"][:],
                                     op0=ALU.mult, op1=ALU.add))
    dve.tensor_scalar(b["var"][:], b["var"][:], EPS, None, ALU.add).then_inc(s["var_ready"], 1)
    dve.wait_ge(s["rstd_ready"], 1)
    with dve.Fori(0, NT // 4) as k:
        for h in range(2):
            q = 2 * k + h
            if rows:
                dve.wait_ge(s[f"rows_out{h}"], 16 * (k + 1))
            for t in range(2):
                i = 2 * q + t
                ins = dve.tensor_scalar(b["xn"][h][:, t, :], c["x"][:, bass.ds(i, 1), :],
                                        b["mean"][:, bass.ds(i, 1)], b["rstd"][:, bass.ds(i, 1)],
                                        ALU.subtract, ALU.mult)
            ins.then_inc(s["xn_ready"], 1)
        for h in range(2):
            q = 2 * k + h
            dve.wait_ge(s["hi_done"], q + 1)
            hi, lo = (w[:, :, bass.ds(q * 2 * P, 2 * P)] for w in xT)
            dve.tensor_tensor(lo, b["bank"][h][:, :].rearrange("p (c t) -> p c t", c=DC), f32(hi),
                              ALU.subtract).then_inc(s["lo_done"], 1)


def norm_pool(pool, c, b, s):
    pool.wait_ge(s["var_ready"], 1)
    pool.tensor_tensor(b["rstd"][:], b["var"][:], c["mhalf"][:], ALU.pow).then_inc(s["rstd_ready"], 1)


def norm_tensor(pe, c, b, s):
    def pairs(k):
        for h in range(2):
            q = 2 * k + h
            pe.wait_ge(s["xn_ready"], q + 1)
            pe.wait_ge(s["lo_done"], 2 * k)
            for t in range(2):
                for d in range(DC):
                    ins = pe.transpose(b["bank"][h][:, d * 2 * P + t * P:d * 2 * P + (t + 1) * P],
                                       b["xn"][h][:, t, d * P:(d + 1) * P], c["ident"][:])
            ins.then_inc(s["turned"], 1)

    pairs(0)
    with pe.Fori(1, NT // 4) as k:
        pairs(k)


def norm_scalar(act, b, s, xT):
    with act.Fori(0, NT // 4) as k:
        for h in range(2):
            q = 2 * k + h
            act.wait_ge(s["turned"], q + 1)
            act.activation(xT[0][:, :, bass.ds(q * 2 * P, 2 * P)],
                           b["bank"][h][:, :].rearrange("p (c t) -> p c t", c=DC), ACT.Copy).then_inc(s["hi_done"], 1)


def norm_rows(sp, b, s, rows):
    for h in range(2):
        sp.sem_inc(s[f"rows_out{h}"], 16)
    view = rows.rearrange("(q t p) r -> q p t r", t=2, p=P)
    with sp.Fori(0, NT // 4) as k:
        for h in range(2):
            q = 2 * k + h
            sp.wait_ge(s["xn_ready"], q + 1)
            sp.dma_start(view[bass.ds(q, 1), :, :, 0:D].rearrange("q p t r -> (q p) t r"),
                         b["xn"][h][:]).then_inc(s[f"rows_out{h}"], 16)
    for h in range(2):
        sp.wait_ge(s[f"rows_out{h}"], 16 + 16 * (NT // 4))


def ffn_shared_and_route(nc, c, r, rows, tok_dram, tag):
    with ExitStack() as ctx:
        m = Memory(nc, ctx, tag)
        xT = [m.sb(f"xT{k}", [P, DC, N], F32R) for k in range(2)]
        nb, ns = norm_buffers(m), norm_sems(m)
        lgT = m.sb("lgT", [E, CH])
        lg = m.sb("lg", [P, K, E])
        lgb = m.sb("lgb", [P, K, E])
        ex = m.sb("ex", [P, K, E])
        score = m.sb("score", [P, K, E])
        mask = m.sb("mask", [P, K, E])
        hot = m.sb("hot", [P, K, E])
        wrow = m.sb("wrow", [P, K, E])
        small = m.sb("small", [P, 5, K])
        best = m.sb("best", [P, K, 8])
        besti = m.sb("besti", [P, K, 8], U32)
        bestf = m.sb("bestf", [P, K, 8])
        keys = m.sb("keys", [E, N])
        first = m.sb("first", [E, CAP])
        tok_e = m.sb("tok_e", [E, CAP])
        tok_g = m.sb("tok_g", [NG, P])
        sil = [m.sb(f"sil{k}", [P, CH]) for k in range(2)]
        hid = [m.sb(f"hid{k}", [P, CH]) for k in range(2)]
        hT = [m.sb(f"hT{k}", [P, SM, CH], F32R) for k in range(2)]
        gate = [m.ps(f"gate{k}") for k in range(2)]
        up = [m.ps(f"up{k}") for k in range(2)]
        down = [m.ps(f"down{k}") for k in range(2)]
        rt = m.ps("rt")
        rl = m.ps("rl")
        nb["bank"] = gate
        sems = ("lgT_done lgT_read lgT_sb lg_done shifted exp_done route mask_ready maskT_done w_ready w_out "
                "gu_done sil_done hid_ready hi_done lo_done down_done x_added keys_done table "
                "tok_ready tok_out tok_in tok_turned rl_read passed")
        q = {n: m.sem(n) for n in sems.split()}
        block = ctx.enter_context(nc.Block())

        def mm3(pe, out, lhs, rhs, first, last):
            pe.matmul(out, lhs[0], rhs[0], start=first, stop=False)
            pe.matmul(out, lhs[0], rhs[1], start=False, stop=False)
            return pe.matmul(out, lhs[1], rhs[0], start=False, stop=last)

        @block.tensor
        def _(pe):
            norm_tensor(pe, c, nb, ns)
            pe.wait_ge(ns["lo_done"], NT // 2)
            def chunk(ch):
                xc = [[w[:, d, bass.ds(ch * CH, CH)] for w in xT] for d in range(DC)]
                pe.wait_ge(q["keys_done"], ch)
                for d in range(DC):
                    ins = mm3(pe, rt[:], [w[:, d, :] for w in c["rw"]], xc[d], d == 0, d == DC - 1)
                ins.then_inc(q["lgT_done"], 1)
                for mi in range(SM):
                    n = ch * SM + mi
                    if mi == 1:
                        pe.wait_ge(q["lgT_sb"], ch + 1)
                        pe.wait_ge(q["rl_read"], ch)
                        apart(pe, q["passed"])
                        for t in range(4):
                            ins = pe.transpose(rl[:, t * E:(t + 1) * E], lgT[:, t * P:(t + 1) * P], c["ident"][0:E, 0:E])
                        ins.then_inc(q["lg_done"], 1)
                    if mi >= 2:
                        pe.wait_ge(q["hid_ready"], n - 1)
                    else:
                        pe.wait_ge(q["hid_ready"], ch * SM)
                    for bank, w in ((gate, "gw"), (up, "uw")):
                        for d in range(DC):
                            ins = mm3(pe, bank[mi % 2][:], [v[:, d, mi * P:(mi + 1) * P] for v in c[w]], xc[d],
                                      d == 0, d == DC - 1)
                    ins.then_inc(q["gu_done"], 1)
                pe.wait_ge(q["mask_ready"], ch + 1)
                apart(pe, q["passed"])
                for t in range(4):
                    ins = pe.transpose(rt[0:E, t * P:(t + 1) * P], mask[:, t, :], c["ident"][:])
                ins.then_inc(q["maskT_done"], 1)
                pe.wait_ge(q["lo_done"], SM * ch + SM)
                for t in range(4):
                    if t % 2 == 0:
                        pe.wait_ge(q["x_added"], 2 * ch)
                    o = down[t // 2][:, (t % 2) * D:(t % 2 + 1) * D]
                    for mi in range(SM):
                        ins = mm3(pe, o, [w[:, mi, t * P:(t + 1) * P] for w in hT], [w[:, mi, :] for w in c["dw"]],
                                  mi == 0, mi == SM - 1)
                    if t % 2 == 1:
                        ins.then_inc(q["down_done"], 1)

            chunk(0)
            with pe.Fori(1, NCH) as ch:
                chunk(ch)
            pe.wait_ge(q["tok_in"], 16)
            pe.transpose(rl[:, 0:NG], tok_g[:], c["ident"][0:NG, 0:NG]).then_inc(q["tok_turned"], 1)

        @block.scalar
        def _(act):
            norm_scalar(act, nb, ns, xT)
            def chunk(ch):
                act.wait_ge(q["lgT_done"], ch + 1)
                act.wait_ge(q["lg_done"], ch)
                act.activation(lgT[:], rt[0:E, :], ACT.Copy).then_inc(q["lgT_sb"], 1)
                for mi in range(SM):
                    n = ch * SM + mi
                    act.wait_ge(q["gu_done"], n + 1)
                    if mi >= 2:
                        act.wait_ge(q["lo_done"], n - 1)
                    else:
                        act.wait_ge(q["lo_done"], ch * SM)
                    act.activation(sil[mi % 2][:], gate[mi % 2][:], ACT.Silu).then_inc(q["sil_done"], 1)
                    act.wait_ge(q["hid_ready"], n + 1)
                    if mi == 0:
                        act.wait_ge(q["down_done"], 2 * ch)
                    act.activation(hT[0][:, mi, :], hid[mi % 2][:], ACT.Copy).then_inc(q["hi_done"], 1)
                    if mi == 1:
                        act.wait_ge(q["shifted"], ch + 1)
                        act.activation(ex[:], ex[:], ACT.Exp).then_inc(q["exp_done"], 1)

            chunk(0)
            with act.Fori(1, NCH) as ch:
                chunk(ch)

        @block.vector
        def _(dve):
            norm_vector(dve, c, nb, ns, xT, True)
            mx, z, rz, s4, rs = (small[:, n, :] for n in range(5))

            def wide(v):
                return v.unsqueeze(2).broadcast_to([P, K, E])

            def hidden(ch, mi):
                n = ch * SM + mi
                dve.wait_ge(q["sil_done"], n + 1)
                dve.tensor_tensor(hid[mi % 2][:], up[mi % 2][:], sil[mi % 2][:], ALU.mult).then_inc(q["hid_ready"], 1)
                dve.wait_ge(q["hi_done"], n + 1)
                dve.tensor_tensor(hT[1][:, mi, :], hid[mi % 2][:], f32(hT[0][:, mi, :]),
                                  ALU.subtract).then_inc(q["lo_done"], 1)

            def chunk(ch):
                ro = Counter(dve, q["route"], ch * ROUTE_STEPS)
                hidden(ch, 0)
                dve.wait_ge(q["lg_done"], ch + 1)
                lgp = rl[:, 0:K * E].rearrange("p (t e) -> p t e", t=K)
                dve.wait_ge(q["exp_done"], ch)
                ro.then(dve.tensor_copy(lg[:], lgp))
                dve.sem_inc(q["rl_read"], 1)
                ro.then(dve.tensor_reduce(mx, lg[:], X, ALU.max))
                dve.tensor_tensor(ex[:], lg[:], wide(mx), ALU.subtract).then_inc(q["shifted"], 1)
                ro.then(dve.tensor_tensor(lgb[:], lg[:], c["rbias"][:].unsqueeze(1).broadcast_to([P, K, E]), ALU.add), q["passed"])
                for t in range(4):
                    ins = dve.max(best[:, t, :], lgb[:, t, :])
                ro.then(ins, q["passed"])
                for t in range(4):
                    ins = dve.max_index(besti[:, t, :], best[:, t, :], lgb[:, t, :])
                ro.then(ins)
                hidden(ch, 1)
                ro.then(dve.tensor_copy(bestf[:], besti[:]))
                io = c["iota_e"][:].unsqueeze(1).broadcast_to([P, K, E])
                dve.wait_ge(q["maskT_done"], ch)
                ro.then(dve.tensor_tensor(mask[:], io, wide(bestf[:, :, 0]), ALU.is_equal))
                for k in range(1, K):
                    ro.then(dve.tensor_tensor(hot[:], io, wide(bestf[:, :, k]), ALU.is_equal))
                    ro.then(dve.tensor_tensor(mask[:], mask[:], hot[:], ALU.add))
                dve.sem_inc(q["mask_ready"], 1)
                hidden(ch, 2)
                dve.wait_ge(q["exp_done"], ch + 1)
                ro.then(dve.tensor_reduce(z, ex[:], X, ALU.add))
                ro.then(dve.reciprocal(rz, z))
                ro.then(dve.tensor_tensor(score[:], ex[:], wide(rz), ALU.mult))
                ro.then(dve.tensor_tensor(score[:], score[:], mask[:], ALU.mult))
                ro.then(dve.tensor_reduce(s4, score[:], X, ALU.add))
                ro.then(dve.reciprocal(rs, s4))
                dve.wait_ge(q["w_out"], 16 * ch)
                ro.then(dve.tensor_tensor(wrow[:], score[:], wide(rs), ALU.mult))
                dve.sem_inc(q["w_ready"], 1)
                hidden(ch, 3)
                dve.wait_ge(q["maskT_done"], ch + 1)
                dve.tensor_tensor(keys[:, bass.ds(ch * CH, CH)], rt[0:E, :], c["down_t"][:, bass.ds(ch * CH, CH)],
                                  ALU.mult).then_inc(q["keys_done"], 1)
                for o in range(2):
                    dve.wait_ge(q["down_done"], 2 * ch + o + 1)
                    xs = c["x"][:, bass.ds(ch * 4 + 2 * o, 2), :].rearrange("p a b -> p (a b)")
                    dve.scalar_tensor_tensor(out=xs, in0=down[o][:], scalar=0.5, in1=xs, op0=ALU.mult,
                                             op1=ALU.add).then_inc(q["x_added"], 1)
                assert ro.n == ROUTE_STEPS

            chunk(0)
            with dve.Fori(1, NCH) as ch:
                chunk(ch)
            dve.wait_ge(q["keys_done"], NCH)
            tb = Counter(dve, q["table"], 0)
            for n in range(CAP // 8):
                tb.then(dve.max(first[:, 8 * n:8 * n + 8], keys[:]))
                if n < CAP // 8 - 1:
                    tb.then(dve.match_replace(keys[:], first[:, 8 * n:8 * n + 8], keys[:], 0.0))
            dve.tensor_scalar(tok_e[:], first[:], -1.0, float(N), ALU.mult, ALU.add).then_inc(q["tok_ready"], 1)
            dve.wait_ge(q["tok_turned"], 1)
            tb.then(dve.tensor_copy(r["tok"][:], rl[:, 0:NG]))
            dve.tensor_scalar(r["tok_i"][:], r["tok"][:], float(N - 1), None, ALU.min)

        @block.gpsimd
        def _(pool):
            norm_pool(pool, c, nb, ns)

        @block.sync
        def _(sp):
            norm_rows(sp, nb, ns, rows)
            wview = rows.rearrange("(c t p) r -> c p t r", t=4, p=P)
            with sp.Fori(0, NCH) as ch:
                sp.wait_ge(q["w_ready"], ch + 1)
                sp.dma_start(wview[bass.ds(ch, 1), :, :, D:ROW].rearrange("c p t r -> (c p) t r"),
                             wrow[:]).then_inc(q["w_out"], 16)
            sp.wait_ge(q["w_out"], 16 * NCH)
            sp.wait_ge(q["tok_ready"], 1)
            sp.dma_start(tok_dram, tok_e[:]).then_inc(q["tok_out"], 16)
            sp.wait_ge(q["tok_out"], 16)
            sp.dma_start(tok_g[:], tok_dram.rearrange("(g e) c -> g (e c)", e=EG)).then_inc(q["tok_in"], 16)
            sp.wait_ge(q["tok_in"], 16)


def ffn_experts(nc, c, r, rows, a, out, tag):
    with ExitStack() as ctx:
        m = Memory(nc, ctx, tag)
        idx = [m.sb(f"idx{s}", [P, 1], I32) for s in range(2)]
        xg = [m.sb(f"xg{s}", [P, ROW]) for s in range(2)]
        raw_g = [m.sb(f"raw_g{s}", [P, 2, D]) for s in range(2)]
        raw_u = [m.sb(f"raw_u{s}", [P, 2, D]) for s in range(2)]
        raw_d = [m.sb(f"raw_d{s}", [P, DC, EG, F]) for s in range(2)]
        guT = [m.sb(f"guT{s}", [P, DC, 2 * EG * F]) for s in range(2)]
        dT = [m.sb(f"dT{s}", [P, 2, D]) for s in range(2)]
        xgT = [m.sb(f"xgT{s}", [P, DC, P]) for s in range(2)]
        sil = [m.sb(f"sil{s}", [P, F]) for s in range(2)]
        hid = [m.sb(f"hid{s}", [P, EG * F]) for s in range(2)]
        hT = [m.sb(f"hT{s}", [P, 2, P]) for s in range(2)]
        wtmp = [m.sb(f"wtmp{s}", [P, E]) for s in range(2)]
        ws = [m.sb(f"ws{s}", [P, 1]) for s in range(2)]
        y = m.sb("y", [P, NG, 2, D], F32R)
        hot = [m.sb(f"hot{s}", [P, NG, P], F32R) for s in range(2)]
        b_gu = [m.ps(f"b_gu{k}") for k in range(DC)]
        b_d, b_x, b_h = m.ps("b_d"), m.ps("b_x"), m.ps("b_h")
        b_act, b_y = m.ps("b_act"), m.ps("b_y")
        sems = ("idx_ready turned sb_gu0 sb_gu1 sb_x sb_d gu_done sil_done hid_ready h_turned sb_h "
                "y_done y_hi y_lo w_step w_ready zeroed hot_ready sum_done x_part x_done stored passed")
        q = {n: m.sem(n) for n in sems.split()}
        raw_in = [m.sem(f"raw_in_slot{s}") for s in range(2)]
        xg_in = [m.sem(f"xg_in_slot{s}") for s in range(2)]
        block = ctx.enter_context(nc.Block())
        sums = [b_act, b_y]

        @block.sync
        def _(sp):
            def load(g, s):
                gu = "e f d -> (e f) d"
                e0 = g * EG
                for dst, name in ((raw_g, "gate_w"), (raw_u, "up_w")):
                    src = a[name][bass.ds(e0, EG), :, :].rearrange(gu).rearrange("(h p) d -> p h d", p=P)
                    sp.dma_start(dst[s][:], src).then_inc(raw_in[s], 16)
                for k in range(DC):
                    src = a["down_w"][bass.ds(e0, EG), k * P:(k + 1) * P, :].rearrange("e p f -> p e f")
                    sp.dma_start(raw_d[s][:, k, :, :], src).then_inc(raw_in[s], 16)

            for s in range(2):
                load(s, s)
            with sp.Fori(1, NG // 2) as k:
                for s in range(2):
                    sp.wait_ge(q["turned"], 2 * k + s - 1)
                    load(2 * k + s, s)
            if out is not None:
                with sp.Fori(0, NT) as i:
                    sp.wait_ge(q["x_done"], i + 1)
                    sp.dma_start(out[bass.ds(i, 1), :, :].rearrange("i p d -> (i p) d"),
                                 c["x"][:, bass.ds(i, 1), :].rearrange("p i d -> p (i d)")).then_inc(q["stored"], 16)
                sp.wait_ge(q["stored"], 16 * NT)

        @block.gpsimd
        def _(pool):
            def gather(g, s, first):
                if not first:
                    pool.wait_ge(q["turned"], g - 1)
                    pool.wait_ge(q["w_ready"], g - 1)
                pool.tensor_copy(idx[s][:], r["tok_i"][:, bass.ds(g, 1)]).then_inc(q["idx_ready"], 1)
                pool.wait_ge(q["idx_ready"], g + 1)
                apart(pool, q["passed"])
                pool.indirect_dma_start(out=xg[s][:], out_offset=None, in_=rows,
                                        in_offset=bass.IndirectOffsetOnAxis(ap=idx[s][:, 0:1], axis=0)
                                        ).then_inc(xg_in[s], 16)

            for s in range(2):
                gather(s, s, True)
            with pool.Fori(1, NG // 2) as k:
                for s in range(2):
                    gather(2 * k + s, s, False)

        @block.tensor
        def _(pe):
            def turn(g, s, nth):
                pe.wait_ge(raw_in[s], 64 * nth)
                pe.wait_ge(q["sb_gu0"], g)
                pe.wait_ge(q["sb_gu1"], g)
                for k in range(DC):
                    for w, raw in enumerate((raw_g, raw_u)):
                        for h in range(2):
                            col = w * EG * F + h * P
                            pe.transpose(b_gu[k][:, col:col + P], raw[s][:, h, k * P:(k + 1) * P], c["ident"][:])
                pe.wait_ge(q["sb_d"], g)
                for h in range(2):
                    for k in range(DC):
                        pe.transpose(b_d[:, h * D + k * P:h * D + (k + 1) * P],
                                     raw_d[s][:, k, 2 * h:2 * h + 2, :].rearrange("p e f -> p (e f)"), c["ident"][:])
                pe.wait_ge(xg_in[s], 16 * nth)
                pe.wait_ge(q["sb_x"], g)
                for k in range(DC):
                    ins = pe.transpose(b_x[:, k * P:(k + 1) * P], xg[s][:, k * P:(k + 1) * P], c["ident"][:])
                ins.then_inc(q["turned"], 1)

            def expert(g, s, more):
                pe.wait_ge(q["sb_gu0"], g + 1)
                pe.wait_ge(q["sb_gu1"], g + 1)
                pe.wait_ge(q["sb_x"], g + 1)
                pe.wait_ge(q["hid_ready"], g)
                for k in range(DC):
                    ins = pe.matmul(b_act[:], xgT[s][:, k, :], guT[s][:, k, :], start=(k == 0), stop=(k == DC - 1))
                ins.then_inc(q["gu_done"], 1)
                if more is not None:
                    turn(g + 1, 1 - s, more)
                pe.wait_ge(q["hid_ready"], g + 1)
                pe.wait_ge(q["sb_h"], g)
                for h in range(2):
                    ins = pe.transpose(b_h[:, h * P:(h + 1) * P], hid[s][:, h * P:(h + 1) * P], c["ident"][:])
                ins.then_inc(q["h_turned"], 1)
                pe.wait_ge(q["sb_h"], g + 1)
                pe.wait_ge(q["sb_d"], g + 1)
                pe.wait_ge(q["y_lo"], g)
                for h in range(2):
                    ins = pe.matmul(b_y[:, 0:D], hT[s][:, h, :], dT[s][:, h, :], start=(h == 0), stop=(h == 1))
                ins.then_inc(q["y_done"], 1)

            turn(0, 0, 1)
            expert(0, 0, 1)
            expert(1, 1, 2)
            with pe.Fori(1, NG // 2 - 1) as k:
                expert(2 * k, 0, k + 1)
                expert(2 * k + 1, 1, k + 2)
            expert(NG - 2, 0, NG // 2)
            expert(NG - 1, 1, None)

            pe.wait_ge(q["y_lo"], NG)
            def collect(i, s, first):
                pe.wait_ge(q["hot_ready"], i + 1)
                if not first:
                    pe.wait_ge(q["x_done"], i - 1)
                for g in range(NG):
                    ins = pe.matmul(sums[s][:], hot[s][:, g, :], y[:, g, :, :].rearrange("p a b -> p (a b)"),
                                    start=(g == 0), stop=(g == NG - 1))
                ins.then_inc(q["sum_done"], 1)

            collect(0, 0, True)
            collect(1, 1, True)
            with pe.Fori(1, NT // 2) as k:
                for s in range(2):
                    collect(2 * k + s, s, False)

        @block.scalar
        def _(act):
            def turned(g, s):
                act.wait_ge(q["turned"], g + 1)
                if not isinstance(g, int) or g >= 2:
                    act.wait_ge(q["gu_done"], g - 1)
                act.activation(guT[s][:, 0, :], b_gu[0][:], ACT.Copy).then_inc(q["sb_gu0"], 1)
                act.activation(xgT[s][:], b_x[:, 0:D].rearrange("p (k t) -> p k t", k=DC),
                               ACT.Copy).then_inc(q["sb_x"], 1)

            def expert(g, s, more):
                act.wait_ge(q["gu_done"], g + 1)
                act.wait_ge(q["sb_gu1"], g + 1)
                for e in range(EG):
                    ps = slice(e * CAP, (e + 1) * CAP)
                    ins = act.activation(sil[s][ps, :], b_act[ps, e * F:(e + 1) * F], ACT.Silu)
                ins.then_inc(q["sil_done"], 1)
                if more:
                    turned(g + 1, 1 - s)
                act.wait_ge(q["h_turned"], g + 1)
                act.activation(hT[s][:], b_h[:, 0:2 * P].rearrange("p (h t) -> p h t", h=2),
                               ACT.Copy).then_inc(q["sb_h"], 1)
                act.wait_ge(q["y_done"], g + 1)
                act.wait_ge(q["w_ready"], g + 1)
                act.activation(y[:, bass.ds(g, 1), 0, :], b_y[:, 0:D], ACT.Copy, scale=ws[s][:, 0:1]).then_inc(q["y_hi"], 1)

            turned(0, 0)
            expert(0, 0, True)
            expert(1, 1, True)
            with act.Fori(1, NG // 2 - 1) as k:
                for s in range(2):
                    expert(2 * k + s, s, True)
            expert(NG - 2, 0, True)
            expert(NG - 1, 1, False)

        @block.vector
        def _(dve):
            for s in range(2):
                dve.memset(hid[s][:], 0.0).then_inc(q["zeroed"], 1)
            dve.wait_ge(q["zeroed"], 2)

            def turned(g, s, first):
                dve.wait_ge(q["turned"], g + 1)
                if not first:
                    dve.wait_ge(q["y_done"], g - 1)
                dve.tensor_copy(guT[s][:, 1, :], b_gu[1][:]).then_inc(q["sb_gu1"], 1)
                dve.tensor_copy(dT[s][:].rearrange("p h d -> p (h d)"), b_d[:]).then_inc(q["sb_d"], 1)
                if not first:
                    dve.wait_ge(q["y_hi"], g - 1)
                dve.tensor_tensor(wtmp[s][:], xg[s][:, D:ROW], c["sel"][:, bass.ds(60 - EG * g, E)],
                                  ALU.mult).then_inc(q["w_step"], 1)
                dve.wait_ge(q["w_step"], g + 1)
                dve.tensor_reduce(ws[s][:], wtmp[s][:], X, ALU.add).then_inc(q["w_ready"], 1)

            def expert(g, s, more, first=False):
                dve.wait_ge(q["sil_done"], g + 1)
                if not first:
                    dve.wait_ge(q["h_turned"], g - 1)
                for e in range(EG):
                    ps = slice(e * CAP, (e + 1) * CAP)
                    ins = dve.tensor_tensor(hid[s][ps, e * F:(e + 1) * F],
                                            b_act[ps, EG * F + e * F:EG * F + (e + 1) * F], sil[s][ps, :], ALU.mult)
                ins.then_inc(q["hid_ready"], 1)
                if more:
                    turned(g + 1, 1 - s, isinstance(g, int) and g + 1 < 2)
                dve.wait_ge(q["y_hi"], g + 1)
                dve.wait_ge(q["w_ready"], g + 1)
                dve.scalar_tensor_tensor(out=y[:, bass.ds(g, 1), 1, :], in0=b_y[:, 0:D], scalar=ws[s][:, 0:1],
                                         in1=f32(y[:, bass.ds(g, 1), 0, :]), op0=ALU.mult,
                                         op1=ALU.subtract).then_inc(q["y_lo"], 1)

            turned(0, 0, True)
            expert(0, 0, True, True)
            expert(1, 1, True, True)
            with dve.Fori(1, NG // 2 - 1) as k:
                for s in range(2):
                    expert(2 * k + s, s, True)
            expert(NG - 2, 0, True)
            expert(NG - 1, 1, False)

            def one_hot(i, s):
                dve.tensor_tensor(hot[s][:], c["iota_t"][:, bass.ds(i * P, P)].unsqueeze(1).broadcast_to([P, NG, P]),
                                  r["tok"][:].unsqueeze(2).broadcast_to([P, NG, P]), ALU.is_equal
                                  ).then_inc(q["hot_ready"], 1)

            def add(i, s):
                dve.wait_ge(q["sum_done"], i + 1)
                xs = c["x"][:, bass.ds(i, 1), :].rearrange("p a b -> p (a b)")
                for h in range(2):
                    ins = dve.scalar_tensor_tensor(out=xs, in0=sums[s][:, h * D:(h + 1) * D], scalar=0.5, in1=xs,
                                                   op0=ALU.mult, op1=ALU.add)
                    if h == 0:
                        ins.then_inc(q["x_part"], 1)
                        dve.wait_ge(q["x_part"], i + 1)
                ins.then_inc(q["x_done"], 1)

            one_hot(0, 0)
            one_hot(1, 1)
            with dve.Fori(0, NT // 2 - 1) as k:
                for s in range(2):
                    add(2 * k + s, s)
                    one_hot(2 * k + s + 2, s)
            for s in range(2):
                add(NT - 2 + s, s)


def attention(nc, c, a, tag):
    with ExitStack() as ctx:
        m = Memory(nc, ctx, tag)
        U = H * B
        xT = [m.sb(f"xT{k}", [P, DC, N], F32R) for k in range(2)]
        nb, ns = norm_buffers(m), norm_sems(m)
        raw_c = m.sb("raw_c", [P, 4, D])
        raw_s = m.sb("raw_s", [P, 4, D])
        w = [[m.sb(f"w{k}_{s}", [P, 4, D], F32R) for k in range(2)] for s in range(2)]
        qT = [[m.sb(f"qT{k}_{s}", [P, S], F32R) for k in range(2)] for s in range(2)]
        kT = [[m.sb(f"kT{k}_{s}", [P, S], F32R) for k in range(2)] for s in range(2)]
        vT = m.sb("vT", [P, S])
        v = [[m.sb(f"v{k}_{s}", [P, 4, HD], F32R) for k in range(2)] for s in range(2)]
        pr = [m.sb(f"pr{s}", [P, 4, S]) for s in range(2)]
        prT = [[m.sb(f"prT{k}_{s}", [P, S], F32R) for k in range(2)] for s in range(2)]
        oT = [[m.sb(f"oT{k}_{s}", [P, S], F32R) for k in range(2)] for s in range(2)]
        junk = [m.sb(f"junk{s}", [P, S], BF16) for s in range(2)]
        nmax = m.sb("nmax", [P, 2, 4])
        rsum = m.sb("rsum", [P, 2, 4])
        rinv = m.sb("rinv", [P, 4, 4])
        b_s = [m.ps(f"b_s{s}") for s in range(2)]
        b_t = [m.ps(f"b_t{s}") for s in range(2)]
        b_o, b_out = m.ps("b_o"), m.ps("b_out")
        b_p = [m.ps(f"b_p{s}") for s in range(2)]
        nb["bank"] = b_s
        sems = ("raw_in w_mul w_hi w_ready bo_added s_done nmax_ready exp_done rinv_ready t_done pt_hi pt_lo pv_done "
                "q_done q_hi q_lo k_done k_hi k_lo vT_done vT_sb v_done v_hi v_lo o_done o_hi o_lo out_done x_added passed")
        q = {n: m.sem(n) for n in sems.split()}
        block = ctx.enter_context(nc.Block())
        LOADS = 11

        def late(t, n):
            return not isinstance(t, int) or t >= n

        def schedule(eng, step):
            for u in range(4):
                step(u, u)
            with eng.Fori(0, 7) as k:
                for j in range(4, 12):
                    step(8 * k + j, j)
            for u in range(60, U):
                step(u, u)

        def later(u, n):
            return not isinstance(u, int) or u + n < U

        @block.sync
        def _(sp):
            def load(h):
                for n, name in enumerate(("wq", "wk", "wv")):
                    sp.dma_start(raw_c[:, n, :].rearrange("p (c f) -> p c f", c=DC),
                                 a[name + "_codes"].rearrange("(c p) f -> p c f", p=P)[:, :, bass.ds(h * HD, HD)]
                                 ).then_inc(q["raw_in"], 16)
                    for k in range(DC):
                        rows = a[name + "_scales"][k * (P // BLK):(k + 1) * (P // BLK), bass.ds(h * HD, HD)]
                        sp.dma_start(raw_s[:, n, k * HD:(k + 1) * HD],
                                     rows.unsqueeze(1).broadcast_to([P // BLK, BLK, HD])).then_inc(q["raw_in"], 16)
                sp.dma_start(raw_c[:, 3, :], a["wo_codes"][bass.ds(h * HD, HD), :]).then_inc(q["raw_in"], 16)
                rows = a["wo_scales"][bass.ds(h * (HD // BLK), HD // BLK), :]
                sp.dma_start(raw_s[:, 3, :], rows.unsqueeze(1).broadcast_to([HD // BLK, BLK, D])).then_inc(q["raw_in"], 16)

            load(0)
            with sp.Fori(1, H) as h:
                sp.wait_ge(q["w_ready"], h)
                load(h)

        @block.gpsimd
        def _(pool):
            def weights(h, s):
                pool.wait_ge(q["raw_in"], 16 * LOADS * (h + 1))
                pool.tensor_tensor(raw_c[:], raw_c[:], raw_s[:], ALU.mult).then_inc(q["w_mul"], 1)
                pool.wait_ge(q["w_mul"], h + 1)
                if late(h, 2):
                    pool.wait_ge(q["out_done"], 2 * B * (h - 1))
                apart(pool, q["passed"])
                pool.tensor_copy(w[s][0][:], raw_c[:]).then_inc(q["w_hi"], 1)
                pool.wait_ge(q["w_hi"], h + 1)
                pool.tensor_tensor(w[s][1][:], raw_c[:], f32(w[s][0][:]), ALU.subtract).then_inc(q["w_ready"], 1)

            norm_pool(pool, c, nb, ns)
            weights(0, 0)
            pool.wait_ge(ns["xn_ready"], NT // 2)
            pool.tensor_tensor(c["x"][:], c["x"][:], c["bo"][:].unsqueeze(1).broadcast_to([P, NT, D]),
                               ALU.add).then_inc(q["bo_added"], 1)
            weights(1, 1)
            with pool.Fori(1, H // 2) as k:
                for s in range(2):
                    weights(2 * k + s, s)

        @block.tensor
        def _(pe):
            def mm3(out, lhs, rhs, first, last):
                pe.matmul(out, lhs[0], rhs[0], start=first, stop=False)
                pe.matmul(out, lhs[0], rhs[1], start=False, stop=False)
                return pe.matmul(out, lhs[1], rhs[0], start=False, stop=last)

            def project(bank, n, j):
                b0, s = (j % 4) * S, (j // 4) % 2
                for d in range(DC):
                    ins = mm3(bank[:], [t[:, n, d * HD:(d + 1) * HD] for t in w[s]], [t[:, d, b0:b0 + S] for t in xT],
                              d == 0, d == DC - 1)
                return ins

            def queries(u, j, hd):
                if j % 4 == 0:
                    pe.wait_ge(q["w_ready"], hd + 1)
                if late(u, 2):
                    pe.wait_ge(q["vT_sb"], u - 1)
                elif u == 1:
                    pe.wait_ge(q["q_lo"], 1)
                project(b_p[0], 0, j).then_inc(q["q_done"], 1)

            def keys(u, j):
                if late(u, 2):
                    pe.wait_ge(q["v_lo"], u - 1)
                elif u == 1:
                    pe.wait_ge(q["k_lo"], 1)
                project(b_p[1], 1, j).then_inc(q["k_done"], 1)

            def values(u, j):
                pe.wait_ge(q["q_lo"], u + 2 if later(u, 1) else U)
                project(b_p[0], 2, j).then_inc(q["vT_done"], 1)

            def turn_values(u):
                pe.wait_ge(q["k_lo"], u + 2 if later(u, 1) else U)
                pe.wait_ge(q["vT_sb"], u + 1)
                for t in range(4):
                    ins = pe.transpose(b_p[1][:, t * P:(t + 1) * P], vT[:, t * P:(t + 1) * P], c["ident"][:])
                ins.then_inc(q["v_done"], 1)

            def scores(u, j, i):
                if i == 0:
                    pe.wait_ge(q["q_lo"], u + 1)
                    pe.wait_ge(q["k_lo"], u + 1)
                if late(4 * u + i if isinstance(u, int) else u, 2):
                    pe.wait_ge(q["exp_done"], 4 * u + i - 1)
                mm3(b_s[i % 2][:], [t[:, i * P:(i + 1) * P] for t in qT[j % 2]], [t[:] for t in kT[j % 2]],
                    True, True).then_inc(q["s_done"], 1)

            def turn_probs(u, j, kb):
                if kb == 0:
                    pe.wait_ge(q["exp_done"], 4 * u + 4)
                if late(4 * u + kb if isinstance(u, int) else u, 2):
                    pe.wait_ge(q["pt_lo"], 4 * u + kb - 1)
                for i in range(4):
                    ins = pe.transpose(b_t[kb % 2][:, i * P:(i + 1) * P], pr[j % 2][:, i, kb * P:(kb + 1) * P],
                                       c["ident"][:])
                ins.then_inc(q["t_done"], 1)

            def probs_values(u, j, kb):
                pe.wait_ge(q["pt_lo"], 4 * u + kb + 1)
                if kb == 0:
                    pe.wait_ge(q["v_lo"], u + 1)
                    pe.wait_ge(q["o_lo"], u)
                ins = mm3(b_o[:], [t[:, kb, :] for t in v[j % 2]], [t[:] for t in prT[kb % 2]], kb == 0, kb == 3)
                ins.then_inc(q["pv_done"], 1)

            def output(u, j, o):
                if o == 0:
                    pe.wait_ge(q["o_lo"], u + 1)
                pe.wait_ge(q["x_added"], 2 * u + o)
                for t in range(2):
                    i = 2 * o + t
                    ins = mm3(b_out[:, t * D:(t + 1) * D], [z[:, i * P:(i + 1) * P] for z in oT[j % 2]],
                              [z[:, 3, :] for z in w[(j // 4) % 2]], True, True)
                ins.then_inc(q["out_done"], 1)

            def step(u, j):
                for i in range(4):
                    turn_probs(u, j, i)
                    if later(u, 1):
                        scores(u + 1, j + 1, i)
                    if i > 0:
                        probs_values(u, j, i - 1)
                    if i == 0 and late(u, 2):
                        output(u - 2, j + 6, 1)
                    if i == 0 and later(u, 2):
                        queries(u + 2, j + 2, (u - j) // 4 + (j + 2) // 4)
                    if i == 1 and later(u, 2):
                        keys(u + 2, j + 2)
                    if i == 2 and later(u, 1):
                        values(u + 1, j + 1)
                    if i == 2 and late(u, 1):
                        output(u - 1, j + 7, 0)
                    if i == 3 and later(u, 1):
                        turn_values(u + 1)
                probs_values(u, j, 3)

            norm_tensor(pe, c, nb, ns)
            pe.wait_ge(ns["lo_done"], NT // 2)
            for u in range(2):
                queries(u, u, 0)
                keys(u, u)
            values(0, 0)
            turn_values(0)
            for i in range(4):
                scores(0, 0, i)
            schedule(pe, step)
            output(U - 2, U - 2, 1)
            for o in range(2):
                output(U - 1, U - 1, o)

        @block.scalar
        def _(act):
            def queries(u, j):
                act.wait_ge(q["q_done"], u + 1)
                if late(u, 2):
                    act.wait_ge(q["s_done"], 4 * (u - 1))
                apart(act, q["passed"])
                act.activation(qT[j % 2][0][:], b_p[0][:], ACT.Identity, bias=bias(c["bq"], u, j)).then_inc(q["q_hi"], 1)

            def keys(u, j):
                act.wait_ge(q["k_done"], u + 1)
                apart(act, q["passed"])
                act.activation(kT[j % 2][0][:], b_p[1][:], ACT.Identity, bias=bias(c["bk"], u, j)).then_inc(q["k_hi"], 1)

            def bias(t, u, j):
                return t[:, bass.ds((u - j) // 4 + j // 4, 1)]

            def values(u, j):
                act.wait_ge(q["vT_done"], u + 1)
                act.wait_ge(q["v_done"], u)
                apart(act, q["passed"])
                act.activation(vT[:], b_p[0][:], ACT.Identity, bias=bias(c["bv"], u, j)).then_inc(q["vT_sb"], 1)

            def turned_values(u, j):
                act.wait_ge(q["v_done"], u + 1)
                if late(u, 1):
                    act.wait_ge(q["pv_done"], 4 * (u - 1))
                act.activation(v[j % 2][0][:].rearrange("p t d -> p (t d)"), b_p[1][:], ACT.Copy).then_inc(q["v_hi"], 1)

            def exps(u, j, i):
                if i == 0 and late(u, 1):
                    act.wait_ge(q["t_done"], 4 * (u - 1))
                    act.wait_ge(q["rinv_ready"], u - 1)
                act.wait_ge(q["nmax_ready"], 4 * u + i + 1)
                act.activation(pr[j % 2][:, i, :], b_s[i % 2][:], ACT.Exp, bias=nmax[:, j % 2, i:i + 1], scale=SCALE,
                               accum_out=rsum[:, j % 2, i:i + 1]).then_inc(q["exp_done"], 1)

            def turned_probs(u, kb):
                act.wait_ge(q["t_done"], 4 * u + kb + 1)
                if late(4 * u + kb if isinstance(u, int) else u, 2):
                    act.wait_ge(q["pv_done"], 4 * u + kb - 1)
                act.activation(prT[kb % 2][0][:], b_t[kb % 2][:], ACT.Copy).then_inc(q["pt_hi"], 1)

            def outputs(u, j):
                act.wait_ge(q["pv_done"], 4 * u + 4)
                if late(u, 2):
                    act.wait_ge(q["out_done"], 2 * (u - 1))
                act.activation(oT[j % 2][0][:], b_o[:], ACT.Copy).then_inc(q["o_hi"], 1)

            def step(u, j):
                if late(u, 1):
                    outputs(u - 1, j + 7)
                for i in range(4):
                    turned_probs(u, i)
                    if i == 0 and late(u, 1):
                        turned_values(u, j)
                    if i == 1 and later(u, 2):
                        queries(u + 2, j + 2)
                    if i == 2 and later(u, 2):
                        keys(u + 2, j + 2)
                    if i == 3 and later(u, 1):
                        values(u + 1, j + 1)
                    if later(u, 1):
                        exps(u + 1, j + 1, i)

            norm_scalar(act, nb, ns, xT)
            for u in range(2):
                queries(u, u)
                keys(u, u)
            values(0, 0)
            turned_values(0, 0)
            for i in range(4):
                exps(0, 0, i)
            schedule(act, step)
            outputs(U - 1, U - 1)

        @block.vector
        def _(dve):
            def low(hi, bank, dst, ready, n, done):
                dve.wait_ge(q[ready], n)
                dve.tensor_tensor(dst, bank, f32(hi), ALU.subtract).then_inc(q[done], 1)

            def low_biased(t, bank, name, b, u, j):
                dve.wait_ge(q[name + "_hi"], u + 1)
                dve.scalar_tensor_tensor(out=t[j % 2][1][:], in0=bank[:], scalar=c[b][:, bass.ds((u - j) // 4 + j // 4, 1)],
                                         in1=f32(t[j % 2][0][:]), op0=ALU.add, op1=ALU.subtract
                                         ).then_inc(q[name + "_lo"], 1)

            def turned_values(u, j):
                hi, lo = (t[:].rearrange("p t d -> p (t d)") for t in v[j % 2])
                low(hi, b_p[1][:], lo, "v_hi", u + 1, "v_lo")

            def maxima(u, j, i):
                dve.wait_ge(q["s_done"], 4 * u + i + 1)
                dve.tensor_scalar(junk[i % 2][:], b_s[i % 2][:], -SCALE, None, ALU.mult, ALU.min,
                                  accum_out=nmax[:, j % 2, i:i + 1]).then_inc(q["nmax_ready"], 1)

            def add(u, j, o):
                dve.wait_ge(q["out_done"], 2 * u + o + 1)
                for t in range(2):
                    i = 2 * o + t
                    xs = c["x"][:, (j % 4) * 4 + i, :]
                    ins = dve.scalar_tensor_tensor(out=xs, in0=b_out[:, t * D:(t + 1) * D],
                                                   scalar=rinv[:, j % 4, i:i + 1], in1=xs, op0=ALU.mult, op1=ALU.add)
                ins.then_inc(q["x_added"], 1)

            def outputs(n, j):
                low(oT[j % 2][0][:], b_o[:], oT[j % 2][1][:], "o_hi", n, "o_lo")

            def step(u, j):
                if late(u, 1):
                    outputs(u, j + 7)
                for i in range(4):
                    low(prT[i % 2][0][:], b_t[i % 2][:], prT[i % 2][1][:], "pt_hi", 4 * u + i + 1, "pt_lo")
                    if later(u, 1):
                        maxima(u + 1, j + 1, i)
                    if i == 0:
                        if late(u, 4):
                            dve.wait_ge(q["x_added"], 2 * (u - 3))
                        dve.reciprocal(rinv[:, j % 4, :], rsum[:, j % 2, :]).then_inc(q["rinv_ready"], 1)
                        if late(u, 1):
                            turned_values(u, j)
                        else:
                            dve.wait_ge(q["bo_added"], 1)
                    if i == 1:
                        if later(u, 2):
                            low_biased(qT, b_p[0], "q", "bq", u + 2, j + 2)
                        if late(u, 2):
                            add(u - 2, j + 6, 1)
                    if i == 2 and later(u, 2):
                        low_biased(kT, b_p[1], "k", "bk", u + 2, j + 2)
                    if i == 3 and late(u, 1):
                        add(u - 1, j + 7, 0)

            norm_vector(dve, c, nb, ns, xT, False)
            for u in range(2):
                low_biased(qT, b_p[0], "q", "bq", u, u)
                low_biased(kT, b_p[1], "k", "bk", u, u)
            turned_values(0, 0)
            for i in range(4):
                maxima(0, 0, i)
            schedule(dve, step)
            outputs(U, U - 1)
            add(U - 2, U - 2, 1)
            for o in range(2):
                add(U - 1, U - 1, o)


def macaron_layer(nc, a, out):
    rows = nc.dram_tensor("rows", (N, ROW), F32).ap()
    tok_dram = nc.dram_tensor("tok_dram", (E, CAP), F32).ap()
    with ExitStack() as ctx:
        m = Memory(nc, ctx, "keep")
        c = prepare(nc, m, a)
        r = dict(tok=m.sb("tok", [P, NG]), tok_i=m.sb("tok_i", [P, NG], I32))
        ffn_shared_and_route(nc, c, r, rows, tok_dram, "f1")
        ffn_experts(nc, c, r, rows, a, None, "e1")
        attention(nc, c, a, "at")
        ffn_shared_and_route(nc, c, r, rows, tok_dram, "f2")
        ffn_experts(nc, c, r, rows, a, out.rearrange("b (i p) d -> (b i) p d", p=P), "e2")


NAMES = [("x", "L0_attn_x")] + [(f"{w}_{t}", f"L0_attn_{w}_{t}") for w in ("wq", "wk", "wv", "wo") for t in ("codes", "scales")] \
    + [(b, f"L0_attn_{b}") for b in ("bq", "bk", "bv", "bo")] \
    + [(f, f"L0_ffn_{f}") for f in ("router_w", "router_bias", "gate_w", "up_w", "down_w", "sh_gate_w", "sh_up_w",
                                    "sh_down_w")]


def kernel(**inputs):
    import concourse.bacc as bacc
    from concourse.bass_utils import run_bass_kernel_spmd

    nc = bacc.Bacc("TRN2", target_bir_lowering=False, num_devices=1)
    arrays, args = {}, {}
    for short, name in NAMES:
        arr = np.ascontiguousarray(inputs[name])
        arrays[f"in_{short}"] = arr
        args[short] = nc.dram_tensor(f"in_{short}", arr.shape, mybir.dt.from_np(arr.dtype), kind="ExternalInput").ap()
    out = nc.dram_tensor("out", (B, S, D), F32, kind="ExternalOutput").ap()
    macaron_layer(nc, args, out)
    result = run_bass_kernel_spmd(nc, [arrays], core_ids=[0])
    return result.results[0]["out"]
```

```python
from contextlib import ExitStack

import numpy as np
import concourse.bass as bass
from concourse import mybir

F32 = mybir.dt.float32
F32R = mybir.dt.float32r
I32 = mybir.dt.int32
U32 = mybir.dt.uint32
BF16 = mybir.dt.bfloat16
ACT = mybir.ActivationFunctionType
ALU = mybir.AluOpType
X = mybir.AxisListType.X

P = 128
D = 256
DC = D // P
N = 2048
NT = N // P
E = 64
K = 4
F = 64
CAP = 32
SH = 512
SM = SH // P
EPS = 1e-5
CH = 512
NCH = N // CH
EG = 4
NG = E // EG
ROW = D + E
H = 16
B = 4
S = 512
HD = 128
FEAT = H * HD
BLK = 32
SCALE = 1.0 / float(np.sqrt(np.float32(HD)))


ROUTE_STEPS = 3 + 2 + 1 + K + 7
TABLE_STEPS = 2 * (CAP // 8)


def f32(ap):
    return ap.bitcast(F32)


def apart(eng, passed):
    eng.sem_inc(passed, 1)


class Counter:

    def __init__(self, eng, sem, base):
        self.eng, self.sem, self.base, self.n = eng, sem, base, 0

    def then(self, ins, passed=None):
        self.count(ins)
        self.wait(passed)

    def count(self, ins):
        self.n += 1
        ins.then_inc(self.sem, 1)

    def wait(self, passed=None):
        self.eng.wait_ge(self.sem, self.base + self.n)
        if passed is not None:
            apart(self.eng, passed)


class Memory:
    def __init__(self, nc, ctx, tag):
        self.nc, self.ctx, self.tag, self.sems = nc, ctx, tag, []

    def sb(self, name, shape, dt=F32):
        return self.ctx.enter_context(self.nc.sbuf_tensor(f"{self.tag}_{name}", shape, dt))

    def ps(self, name, shape=(P, 512), dt=F32):
        return self.ctx.enter_context(self.nc.psum_tensor(f"{self.tag}_{name}", list(shape), dt))

    def sem(self, name):
        if not self.sems:
            self.ctx.callback(self.clear)
        self.sems.append(self.nc.alloc_semaphore(name=f"{self.tag}_{name}"))
        return self.sems[-1]

    def clear(self):
        self.nc.clear_and_free_semaphores(self.sems)
        self.nc.all_engine_barrier()


def prepare(nc, m, a):
    c = dict(
        x=m.sb("x", [P, NT, D]), ident=m.sb("ident", [P, P]),
        iota_e=m.sb("iota_e", [P, E]), iota_t=m.sb("iota_t", [P, N]), down_t=m.sb("down_t", [E, N]),
        sel=m.sb("sel", [P, 124]), mhalf=m.sb("mhalf", [P, NT]),
        rbias=m.sb("rbias", [P, E]), bo=m.sb("bo", [P, D]),
        bq=m.sb("bq", [P, H]), bk=m.sb("bk", [P, H]), bv=m.sb("bv", [P, H]),
        rw=[m.sb(f"rw{k}", [P, DC, P], F32R) for k in range(2)],
        gw=[m.sb(f"gw{k}", [P, DC, SH], F32R) for k in range(2)],
        uw=[m.sb(f"uw{k}", [P, DC, SH], F32R) for k in range(2)],
        dw=[m.sb(f"dw{k}", [P, SM, D], F32R) for k in range(2)],
    )
    with ExitStack() as ctx:
        t = Memory(nc, ctx, "prep")
        raw_g = t.sb("raw_g", [P, SM, D])
        raw_u = t.sb("raw_u", [P, SM, D])
        raw_d = t.sb("raw_d", [P, 2, DC, D])
        raw_r = t.sb("raw_r", [E, D])
        raw_b = t.sb("raw_b", [H, 3, HD])
        banks = [t.ps(f"bank{k}") for k in range(2)]
        loaded, x_loaded, consts, zeroed = (t.sem(n) for n in ("loaded", "x_loaded", "consts", "zeroed"))
        turned, hi_done, lo_done = t.sem("turned"), t.sem("hi_done"), t.sem("lo_done")
        block = ctx.enter_context(nc.Block())
        n_loads = 10

        @block.sync
        def _(sp):
            sp.dma_start(raw_g[:], a["sh_gate_w"].rearrange("s (m p) d -> p (s m) d", p=P)).then_inc(loaded, 16)
            sp.dma_start(raw_u[:], a["sh_up_w"].rearrange("s (m p) d -> p (s m) d", p=P)).then_inc(loaded, 16)
            for s in range(2):
                sp.dma_start(raw_d[:, s, :, :], a["sh_down_w"][s].rearrange("(c p) f -> p c f", p=P)).then_inc(loaded, 16)
            sp.dma_start(raw_r[:], a["router_w"]).then_inc(loaded, 16)
            for i, b in enumerate(("bq", "bk", "bv")):
                sp.dma_start(raw_b[:, i, :], a[b].rearrange("(h d) -> h d", d=HD)).then_inc(loaded, 16)
            sp.dma_start(c["rbias"][:], a["router_bias"].partition_broadcast(P)).then_inc(loaded, 16)
            sp.dma_start(c["bo"][:], a["bo"].partition_broadcast(P)).then_inc(loaded, 16)
            sp.dma_start(c["x"][:], a["x"].rearrange("b (i p) d -> p (b i) d", p=P)).then_inc(x_loaded, 16)
            sp.wait_ge(x_loaded, 16)

        @block.gpsimd
        def _(pool):
            pool.memset(c["ident"][:], 0.0).then_inc(consts, 1)
            pool.wait_ge(consts, 1)
            pool.affine_select(out=c["ident"][:], in_=c["ident"][:], compare_op=ALU.not_equal, fill=1.0,
                               base=0, pattern=[[-1, P]], channel_multiplier=1).then_inc(consts, 1)
            pool.iota(c["iota_e"][:], [[1, E]], base=0, channel_multiplier=0,
                      allow_small_or_imprecise_dtypes=True).then_inc(consts, 1)
            pool.iota(c["iota_t"][:], [[1, N]], base=0, channel_multiplier=0,
                      allow_small_or_imprecise_dtypes=True).then_inc(consts, 1)
            pool.iota(c["down_t"][:], [[-1, N]], base=N, channel_multiplier=0,
                      allow_small_or_imprecise_dtypes=True).then_inc(consts, 1)

        jobs = []
        for raw, dst in ((raw_g, "gw"), (raw_u, "uw")):
            for k in range(DC):
                jobs.append(([raw[:, i, k * P:(k + 1) * P] for i in range(SM)], [w[:, k, :] for w in c[dst]], P))
        for s in range(2):
            jobs.append(([raw_d[:, s, k, i * P:(i + 1) * P] for i in range(2) for k in range(DC)],
                         [w[:, 2 * s:2 * s + 2, :].rearrange("p a b -> p (a b)") for w in c["dw"]], P))
        jobs.append(([raw_r[:, k * P:(k + 1) * P] for k in range(DC)], None, E))
        jobs.append(([raw_b[:, i, :] for i in range(3)], None, H))

        @block.tensor
        def _(pe):
            pe.wait_ge(loaded, 16 * n_loads)
            pe.wait_ge(consts, 2)
            for n, (src, dst, w) in enumerate(jobs):
                if n >= 2:
                    pe.wait_ge(lo_done, n - 1)
                for i, s in enumerate(src):
                    last = pe.transpose(banks[n % 2][:, i * w:(i + 1) * w], s, c["ident"][0:w, 0:w])
                last.then_inc(turned, 1)

        @block.scalar
        def _(act):
            for n, (src, dst, w) in enumerate(jobs):
                act.wait_ge(turned, n + 1)
                bank = banks[n % 2]
                if dst is not None:
                    act.activation(dst[0], bank[:], ACT.Copy).then_inc(hi_done, 1)
                elif w == E:
                    v = bank[:, 0:DC * E].rearrange("p (k e) -> p k e", k=DC)
                    act.activation(c["rw"][0][:, :, 0:E], v, ACT.Copy).then_inc(hi_done, 1)
                else:
                    act.activation(c["bq"][:], bank[:, 0:H], ACT.Copy)
                    act.activation(c["bk"][:], bank[:, H:2 * H], ACT.Copy)
                    act.activation(c["bv"][:], bank[:, 2 * H:3 * H], ACT.Copy).then_inc(hi_done, 1)

        @block.vector
        def _(dve):
            for w in c["rw"]:
                dve.memset(f32(w[:, :, E:P]), 0.0)
            dve.memset(c["mhalf"][:], -0.5)
            dve.memset(c["sel"][:], 0.0).then_inc(zeroed, 1)
            dve.wait_ge(zeroed, 1)
            for q in range(EG):
                dve.memset(c["sel"][q * CAP:(q + 1) * CAP, 60 + q:61 + q], 1.0)
            for n, (src, dst, w) in enumerate(jobs):
                dve.wait_ge(hi_done, n + 1)
                bank = banks[n % 2]
                if dst is not None:
                    dve.tensor_tensor(dst[1], bank[:], f32(dst[0]), ALU.subtract).then_inc(lo_done, 1)
                elif w == E:
                    v = bank[:, 0:DC * E].rearrange("p (k e) -> p k e", k=DC)
                    dve.tensor_tensor(c["rw"][1][:, :, 0:E], v, f32(c["rw"][0][:, :, 0:E]),
                                      ALU.subtract).then_inc(lo_done, 1)
    return c


def norm_sems(m):
    names = "stats moments var_ready rstd_ready xn_ready turned hi_done lo_done rows_out0 rows_out1"
    return {n: m.sem(f"ln_{n}") for n in names.split()}


def norm_buffers(m):
    return dict(stats=m.sb("ln_stats", [P, NT, 6]), mean=m.sb("ln_mean", [P, NT]), var=m.sb("ln_var", [P, NT]),
                tmp=m.sb("ln_tmp", [P, NT]), rstd=m.sb("ln_rstd", [P, NT]),
                xn=[m.sb(f"ln_xn{s}", [P, 2, D]) for s in range(2)])


def norm_vector(dve, c, b, s, xT, rows):
    with dve.Fori(0, NT // 4) as k:
        for t in range(4):
            i = 4 * k + t
            dve.bn_stats(b["stats"][:, bass.ds(i, 1), :], c["x"][:, bass.ds(i, 1), :]).then_inc(s["stats"], 1)
    dve.wait_ge(s["stats"], NT)
    st = b["stats"]
    mo = Counter(dve, s["moments"], 0)
    mo.then(dve.tensor_tensor(b["mean"][:], st[:, :, 1], st[:, :, 4], ALU.add))
    mo.then(dve.tensor_scalar(b["mean"][:], b["mean"][:], 0.5, None, ALU.mult))
    mo.then(dve.tensor_tensor(b["tmp"][:], st[:, :, 1], st[:, :, 4], ALU.subtract))
    mo.then(dve.scalar_tensor_tensor(out=b["tmp"][:], in0=b["tmp"][:], scalar=0.25, in1=b["tmp"][:],
                                     op0=ALU.mult, op1=ALU.mult))
    mo.then(dve.tensor_tensor(b["var"][:], st[:, :, 2], st[:, :, 5], ALU.add))
    mo.then(dve.scalar_tensor_tensor(out=b["var"][:], in0=b["var"][:], scalar=1.0 / D, in1=b["tmp"][:],
                                     op0=ALU.mult, op1=ALU.add))
    dve.tensor_scalar(b["var"][:], b["var"][:], EPS, None, ALU.add).then_inc(s["var_ready"], 1)
    dve.wait_ge(s["rstd_ready"], 1)

    def normalise(k, h):
        if rows:
            dve.wait_ge(s[f"rows_out{h}"], 16 * (k + 1))
        for t in range(2):
            i = 4 * k + 2 * h + t
            ins = dve.tensor_scalar(b["xn"][h][:, t, :], c["x"][:, bass.ds(i, 1), :],
                                    b["mean"][:, bass.ds(i, 1)], b["rstd"][:, bass.ds(i, 1)],
                                    ALU.subtract, ALU.mult)
        ins.then_inc(s["xn_ready"], 1)

    def low(k, h):
        q = 2 * k + h
        dve.wait_ge(s["hi_done"], q + 1)
        hi, lo = (w[:, :, bass.ds(q * 2 * P, 2 * P)] for w in xT)
        dve.tensor_tensor(lo, b["bank"][h][:, :].rearrange("p (c t) -> p c t", c=DC), f32(hi),
                          ALU.subtract).then_inc(s["lo_done"], 1)

    for h in range(2):
        normalise(0, h)
    with dve.Fori(0, NT // 4 - 1) as k:
        for h in range(2):
            dve.wait_ge(s["turned"], 2 * k + h + 1)
            normalise(k + 1, h)
            low(k, h)
    for h in range(2):
        low(NT // 4 - 1, h)


def norm_pool(pool, c, b, s):
    pool.wait_ge(s["var_ready"], 1)
    pool.tensor_tensor(b["rstd"][:], b["var"][:], c["mhalf"][:], ALU.pow).then_inc(s["rstd_ready"], 1)


def norm_tensor(pe, c, b, s):
    def pairs(k):
        for h in range(2):
            q = 2 * k + h
            pe.wait_ge(s["xn_ready"], q + 1)
            if not isinstance(k, int):
                pe.wait_ge(s["lo_done"], q - 1)
            for t in range(2):
                for d in range(DC):
                    ins = pe.transpose(b["bank"][h][:, d * 2 * P + t * P:d * 2 * P + (t + 1) * P],
                                       b["xn"][h][:, t, d * P:(d + 1) * P], c["ident"][:])
            ins.then_inc(s["turned"], 1)

    pairs(0)
    with pe.Fori(1, NT // 4) as k:
        pairs(k)


def norm_scalar(act, b, s, xT):
    with act.Fori(0, NT // 4) as k:
        for h in range(2):
            q = 2 * k + h
            act.wait_ge(s["turned"], q + 1)
            act.activation(xT[0][:, :, bass.ds(q * 2 * P, 2 * P)],
                           b["bank"][h][:, :].rearrange("p (c t) -> p c t", c=DC), ACT.Copy).then_inc(s["hi_done"], 1)


def norm_rows(sp, b, s, rows):
    for h in range(2):
        sp.sem_inc(s[f"rows_out{h}"], 16)
    view = rows.rearrange("(q t p) r -> q p t r", t=2, p=P)
    with sp.Fori(0, NT // 4) as k:
        for h in range(2):
            q = 2 * k + h
            sp.wait_ge(s["xn_ready"], q + 1)
            sp.dma_start(view[bass.ds(q, 1), :, :, 0:D].rearrange("q p t r -> (q p) t r"),
                         b["xn"][h][:]).then_inc(s[f"rows_out{h}"], 16)
    for h in range(2):
        sp.wait_ge(s[f"rows_out{h}"], 16 + 16 * (NT // 4))


def ffn_shared_and_route(nc, c, r, rows, tok_dram, tag):
    with ExitStack() as ctx:
        m = Memory(nc, ctx, tag)
        xT = [m.sb(f"xT{k}", [P, DC, N], F32R) for k in range(2)]
        nb, ns = norm_buffers(m), norm_sems(m)
        lgT = m.sb("lgT", [E, CH])
        lg = m.sb("lg", [P, K, E])
        lgb = m.sb("lgb", [P, K, E])
        ex = m.sb("ex", [P, K, E])
        score = m.sb("score", [P, K, E])
        mask = m.sb("mask", [P, K, E])
        wrow = m.sb("wrow", [P, K, E])
        small = m.sb("small", [P, 5, K])
        best = m.sb("best", [P, K, 8])
        besti = m.sb("besti", [P, K, 8], U32)
        bestf = m.sb("bestf", [P, K, 8])
        keys = m.sb("keys", [E, CAP + CH])
        first_keys = m.sb("first_keys", [E, CAP])
        tok_e = m.sb("tok_e", [E, CAP])
        tok_g = m.sb("tok_g", [NG, P])
        sil = [m.sb(f"sil{k}", [P, CH]) for k in range(2)]
        hid = [m.sb(f"hid{k}", [P, CH]) for k in range(2)]
        hT = [m.sb(f"hT{k}", [P, SM, CH], F32R) for k in range(2)]
        gate = [m.ps(f"gate{k}") for k in range(2)]
        up = [m.ps(f"up{k}") for k in range(2)]
        down = [m.ps(f"down{k}") for k in range(2)]
        rt = m.ps("rt")
        rl = m.ps("rl")
        nb["bank"] = gate
        sems = ("lgT_done lgT_read lgT_sb lg_done shifted exp_done route mask_ready maskT_done w_ready w_out "
                "gu_done sil_done hid_ready hi_done lo_done lo_last down_done x_added keys_done table "
                "tok_ready tok_out tok_in tok_turned tok_kept rl_read passed")
        q = {n: m.sem(n) for n in sems.split()}
        block = ctx.enter_context(nc.Block())

        def mm3(pe, out, lhs, rhs, first, last):
            pe.matmul(out, lhs[0], rhs[0], start=first, stop=False)
            pe.matmul(out, lhs[0], rhs[1], start=False, stop=False)
            return pe.matmul(out, lhs[1], rhs[0], start=False, stop=last)

        @block.tensor
        def _(pe):
            norm_tensor(pe, c, nb, ns)
            pe.wait_ge(ns["lo_done"], NT // 2)

            def gate_up(ch, mi, xc):
                n = ch * SM + mi
                if not isinstance(n, int) or n >= 2:
                    pe.wait_ge(q["hid_ready"], n - 1)
                for bank, w in ((gate, "gw"), (up, "uw")):
                    for d in range(DC):
                        ins = mm3(pe, bank[mi % 2][:], [v[:, d, mi * P:(mi + 1) * P] for v in c[w]], xc[d],
                                  d == 0, d == DC - 1)
                ins.then_inc(q["gu_done"], 1)

            def shared_down(nth):
                pe.wait_ge(q["lo_done"], (SM - 1) * nth)
                pe.wait_ge(q["lo_last"], nth)
                pe.wait_ge(q["x_added"], 2 * nth)
                for t in range(4):
                    o = down[t // 2][:, (t % 2) * D:(t % 2 + 1) * D]
                    for mi in range(SM):
                        ins = mm3(pe, o, [w[:, mi, t * P:(t + 1) * P] for w in hT], [w[:, mi, :] for w in c["dw"]],
                                  mi == 0, mi == SM - 1)
                    if t % 2 == 1:
                        ins.then_inc(q["down_done"], 1)

            def chunk(ch, first=False):
                xc = [[w[:, d, bass.ds(ch * CH, CH)] for w in xT] for d in range(DC)]
                pe.wait_ge(q["keys_done"], ch)
                for d in range(DC):
                    ins = mm3(pe, rt[:], [w[:, d, :] for w in c["rw"]], xc[d], d == 0, d == DC - 1)
                ins.then_inc(q["lgT_done"], 1)
                gate_up(ch, 0, xc)
                pe.wait_ge(q["lgT_sb"], ch + 1)
                pe.wait_ge(q["rl_read"], ch)
                apart(pe, q["passed"])
                for t in range(4):
                    ins = pe.transpose(rl[:, t * E:(t + 1) * E], lgT[:, t * P:(t + 1) * P], c["ident"][0:E, 0:E])
                ins.then_inc(q["lg_done"], 1)
                if not first:
                    shared_down(ch)
                gate_up(ch, 1, xc)
                gate_up(ch, 2, xc)
                pe.wait_ge(q["mask_ready"], ch + 1)
                apart(pe, q["passed"])
                for t in range(4):
                    ins = pe.transpose(rt[0:E, t * P:(t + 1) * P], mask[:, t, :], c["ident"][:])
                ins.then_inc(q["maskT_done"], 1)
                gate_up(ch, 3, xc)

            chunk(0, True)
            with pe.Fori(1, NCH) as ch:
                chunk(ch)
            shared_down(NCH)
            pe.wait_ge(q["tok_in"], 16)
            pe.transpose(rl[:, 0:NG], tok_g[:], c["ident"][0:NG, 0:NG]).then_inc(q["tok_turned"], 1)

        @block.scalar
        def _(act):
            norm_scalar(act, nb, ns, xT)

            def chunk(ch, first=False):
                act.wait_ge(q["lgT_done"], ch + 1)
                act.wait_ge(q["lg_done"], ch)
                act.activation(lgT[:], rt[0:E, :], ACT.Copy).then_inc(q["lgT_sb"], 1)
                for mi in range(SM):
                    n = ch * SM + mi
                    act.wait_ge(q["gu_done"], n + 1)
                    if not first or mi >= 2:
                        act.wait_ge(q["hid_ready"], n - 1)
                    act.activation(sil[mi % 2][:], gate[mi % 2][:], ACT.Silu).then_inc(q["sil_done"], 1)
                    if mi == 0:
                        act.wait_ge(q["shifted"], ch + 1)
                        act.activation(ex[:], ex[:], ACT.Exp).then_inc(q["exp_done"], 1)
                    act.wait_ge(q["hid_ready"], n + 1)
                    if mi == 0:
                        act.wait_ge(q["down_done"], 2 * ch)
                    act.activation(hT[0][:, mi, :], hid[mi % 2][:], ACT.Copy).then_inc(q["hi_done"], 1)

            chunk(0, True)
            with act.Fori(1, NCH) as ch:
                chunk(ch)

        @block.vector
        def _(dve):
            norm_vector(dve, c, nb, ns, xT, True)
            mx, z, rz, s4, rs = (small[:, n, :] for n in range(5))

            def wide(v):
                return v.unsqueeze(2).broadcast_to([P, K, E])

            def hidden(ch, mi, first):
                n = ch * SM + mi
                dve.wait_ge(q["sil_done"], n + 1)
                if mi >= 2:
                    dve.wait_ge(q["lo_done"], (SM - 1) * ch + mi - 1)
                elif not first and mi == 0:
                    dve.wait_ge(q["lo_done"], (SM - 1) * ch)
                elif not first:
                    dve.wait_ge(q["lo_last"], ch)
                dve.tensor_tensor(hid[mi % 2][:], up[mi % 2][:], sil[mi % 2][:], ALU.mult).then_inc(q["hid_ready"], 1)

            def add_shared(ch):
                for o in range(2):
                    dve.wait_ge(q["down_done"], 2 * ch + o + 1)
                    xs = c["x"][:, bass.ds(ch * 4 + 2 * o, 2), :].rearrange("p a b -> p (a b)")
                    dve.scalar_tensor_tensor(out=xs, in0=down[o][:], scalar=0.5, in1=xs, op0=ALU.mult,
                                             op1=ALU.add).then_inc(q["x_added"], 1)

            def best_keys(n):
                return dve.max(first_keys[:, 8 * n:8 * n + 8], keys[:])

            def drop_keys(n):
                return dve.match_replace(keys[:], first_keys[:, 8 * n:8 * n + 8], keys[:], 0.0)

            def chunk(ch, first=False):
                ro = Counter(dve, q["route"], ch * ROUTE_STEPS)
                dve.wait_ge(q["lg_done"], ch + 1)
                lgp = rl[:, 0:K * E].rearrange("p (t e) -> p t e", t=K)
                dve.wait_ge(q["exp_done"], ch)
                ro.then(dve.tensor_copy(lg[:], lgp))
                dve.sem_inc(q["rl_read"], 1)
                ro.then(dve.tensor_reduce(mx, lg[:], X, ALU.max))
                dve.tensor_tensor(ex[:], lg[:], wide(mx), ALU.subtract).then_inc(q["shifted"], 1)
                hidden(ch, 0, first)
                ro.then(dve.tensor_tensor(lgb[:], lg[:], c["rbias"][:].unsqueeze(1).broadcast_to([P, K, E]), ALU.add), q["passed"])
                for t in range(4):
                    ins = dve.max(best[:, t, :], lgb[:, t, :])
                ro.then(ins, q["passed"])
                for t in range(4):
                    ins = dve.max_index(besti[:, t, :], best[:, t, :], lgb[:, t, :])
                ro.then(ins)
                ro.then(dve.tensor_copy(bestf[:], besti[:]))
                dve.wait_ge(q["maskT_done"], ch)
                for k in range(K):
                    for t in range(4):
                        if k == 0:
                            ins = dve.tensor_scalar(mask[:, t, :], c["iota_e"][:], bestf[:, t, k:k + 1], None, ALU.is_equal)
                        else:
                            ins = dve.scalar_tensor_tensor(out=mask[:, t, :], in0=c["iota_e"][:],
                                                           scalar=bestf[:, t, k:k + 1], in1=mask[:, t, :],
                                                           op0=ALU.is_equal, op1=ALU.add)
                    ro.then(ins)
                dve.sem_inc(q["mask_ready"], 1)
                if not first:
                    add_shared(ch - 1)
                hidden(ch, 1, first)
                dve.wait_ge(q["exp_done"], ch + 1)
                tb = None if first else Counter(dve, q["table"], (ch - 1) * TABLE_STEPS + 1 + TABLE_STEPS // 2)
                ro.count(dve.tensor_reduce(z, ex[:], X, ALU.add))
                if tb:
                    apart(dve, q["passed"])
                    tb.count(best_keys(2))
                ro.wait()
                ro.count(dve.reciprocal(rz, z))
                if tb:
                    tb.wait(q["passed"])
                    tb.count(drop_keys(2))
                ro.wait()
                ro.count(dve.tensor_tensor(score[:], ex[:], wide(rz), ALU.mult))
                if tb:
                    tb.wait(q["passed"])
                    tb.count(best_keys(3))
                ro.wait()
                ro.count(dve.tensor_tensor(score[:], score[:], mask[:], ALU.mult))
                if tb:
                    tb.wait()
                    tb.count(dve.tensor_copy(keys[:, 0:CAP], first_keys[:]))
                ro.wait()
                ro.then(dve.tensor_reduce(s4, score[:], X, ALU.add))
                ro.then(dve.reciprocal(rs, s4))
                dve.wait_ge(q["w_out"], 16 * ch)
                ro.then(dve.tensor_tensor(wrow[:], score[:], wide(rs), ALU.mult))
                if tb:
                    tb.wait()
                dve.sem_inc(q["w_ready"], 1)
                dve.wait_ge(q["maskT_done"], ch + 1)
                dve.tensor_tensor(keys[:, CAP:], rt[0:E, :], c["down_t"][:, bass.ds(ch * CH, CH)],
                                  ALU.mult).then_inc(q["keys_done"], 1)
                hidden(ch, 2, first)
                hidden(ch, 3, first)
                dve.wait_ge(q["keys_done"], ch + 1)
                apart(dve, q["passed"])
                tb = Counter(dve, q["table"], 1 + ch * TABLE_STEPS)
                tb.count(best_keys(0))
                dve.wait_ge(q["hi_done"], SM * ch + SM)
                dve.tensor_tensor(hT[1][:, SM - 1, :], hid[1][:], f32(hT[0][:, SM - 1, :]),
                                  ALU.subtract).then_inc(q["lo_last"], 1)
                tb.wait(q["passed"])
                tb.then(drop_keys(0), q["passed"])
                tb.then(best_keys(1), q["passed"])
                tb.then(drop_keys(1), q["passed"])
                assert ro.n == ROUTE_STEPS

            dve.memset(keys[:, 0:CAP], 0.0).then_inc(q["table"], 1)
            dve.wait_ge(q["table"], 1)
            dve.sem_inc(q["x_added"], 2)
            chunk(0, True)
            with dve.Fori(1, NCH) as ch:
                chunk(ch)
            tb = Counter(dve, q["table"], (NCH - 1) * TABLE_STEPS + 1 + TABLE_STEPS // 2)
            tb.then(best_keys(2))
            tb.then(drop_keys(2))
            tb.then(best_keys(3))
            dve.tensor_scalar(tok_e[:], first_keys[:], -1.0, float(N), ALU.mult, ALU.add).then_inc(q["tok_ready"], 1)
            add_shared(NCH - 1)
            dve.wait_ge(q["tok_turned"], 1)
            dve.tensor_copy(r["tok"][:], rl[:, 0:NG]).then_inc(q["tok_kept"], 1)
            dve.wait_ge(q["tok_kept"], 1)
            dve.tensor_scalar(r["tok_i"][:], r["tok"][:], float(N - 1), None, ALU.min)

        @block.gpsimd
        def _(pool):
            norm_pool(pool, c, nb, ns)
            with pool.Fori(0, NCH) as ch:
                for mi in range(SM - 1):
                    pool.wait_ge(q["hi_done"], ch * SM + mi + 1)
                    pool.tensor_tensor(hT[1][:, mi, :], hid[mi % 2][:], f32(hT[0][:, mi, :]),
                                       ALU.subtract).then_inc(q["lo_done"], 1)

        @block.sync
        def _(sp):
            norm_rows(sp, nb, ns, rows)
            wview = rows.rearrange("(c t p) r -> c p t r", t=4, p=P)
            with sp.Fori(0, NCH) as ch:
                sp.wait_ge(q["w_ready"], ch + 1)
                sp.dma_start(wview[bass.ds(ch, 1), :, :, D:ROW].rearrange("c p t r -> (c p) t r"),
                             wrow[:]).then_inc(q["w_out"], 16)
            sp.wait_ge(q["w_out"], 16 * NCH)
            sp.wait_ge(q["tok_ready"], 1)
            sp.dma_start(tok_dram, tok_e[:]).then_inc(q["tok_out"], 16)
            sp.wait_ge(q["tok_out"], 16)
            sp.dma_start(tok_g[:], tok_dram.rearrange("(g e) c -> g (e c)", e=EG)).then_inc(q["tok_in"], 16)
            sp.wait_ge(q["tok_in"], 16)


def ffn_experts(nc, c, r, rows, a, out, tag):
    with ExitStack() as ctx:
        m = Memory(nc, ctx, tag)
        idx = [m.sb(f"idx{s}", [P, 1], I32) for s in range(2)]
        xg = [m.sb(f"xg{s}", [P, ROW]) for s in range(2)]
        raw_g = [m.sb(f"raw_g{s}", [P, 2, D]) for s in range(2)]
        raw_u = [m.sb(f"raw_u{s}", [P, 2, D]) for s in range(2)]
        raw_d = [m.sb(f"raw_d{s}", [P, DC, EG, F]) for s in range(2)]
        guT = [m.sb(f"guT{s}", [P, DC, 2 * EG * F]) for s in range(2)]
        dT = [m.sb(f"dT{s}", [P, 2, D]) for s in range(2)]
        xgT = [m.sb(f"xgT{s}", [P, DC, P]) for s in range(2)]
        sil = [m.sb(f"sil{s}", [P, F]) for s in range(2)]
        hid = [m.sb(f"hid{s}", [P, EG * F]) for s in range(2)]
        hT = [m.sb(f"hT{s}", [P, 2, P]) for s in range(2)]
        wtmp = [m.sb(f"wtmp{s}", [P, E]) for s in range(2)]
        ws = [m.sb(f"ws{s}", [P, 1]) for s in range(2)]
        y = m.sb("y", [P, NG, 2, D], F32R)
        hot = [m.sb(f"hot{s}", [P, NG, P], F32R) for s in range(2)]
        b_gu = [m.ps(f"b_gu{k}") for k in range(DC)]
        b_d, b_x, b_h = m.ps("b_d"), m.ps("b_x"), m.ps("b_h")
        b_act, b_y = m.ps("b_act"), m.ps("b_y")
        sems = ("idx_ready turned sb_gu0 sb_gu1 sb_x sb_d gu_done sil_done hid_ready h_turned sb_h "
                "y_done y_hi y_lo w_step w_ready zeroed hot_ready sum_done x_part x_done stored passed")
        q = {n: m.sem(n) for n in sems.split()}
        raw_in = [m.sem(f"raw_in_slot{s}") for s in range(2)]
        xg_in = [m.sem(f"xg_in_slot{s}") for s in range(2)]
        block = ctx.enter_context(nc.Block())
        sums = [b_act, b_y]

        @block.sync
        def _(sp):
            def load(g, s):
                gu = "e f d -> (e f) d"
                e0 = g * EG
                for dst, name in ((raw_g, "gate_w"), (raw_u, "up_w")):
                    src = a[name][bass.ds(e0, EG), :, :].rearrange(gu).rearrange("(h p) d -> p h d", p=P)
                    sp.dma_start(dst[s][:], src).then_inc(raw_in[s], 16)
                for k in range(DC):
                    src = a["down_w"][bass.ds(e0, EG), k * P:(k + 1) * P, :].rearrange("e p f -> p e f")
                    sp.dma_start(raw_d[s][:, k, :, :], src).then_inc(raw_in[s], 16)

            for s in range(2):
                load(s, s)
            with sp.Fori(1, NG // 2) as k:
                for s in range(2):
                    sp.wait_ge(q["turned"], 2 * k + s - 1)
                    load(2 * k + s, s)
            if out is not None:
                with sp.Fori(0, NT) as i:
                    sp.wait_ge(q["x_done"], i + 1)
                    sp.dma_start(out[bass.ds(i, 1), :, :].rearrange("i p d -> (i p) d"),
                                 c["x"][:, bass.ds(i, 1), :].rearrange("p i d -> p (i d)")).then_inc(q["stored"], 16)
                sp.wait_ge(q["stored"], 16 * NT)

        @block.gpsimd
        def _(pool):
            def gather(g, s, first):
                if not first:
                    pool.wait_ge(q["turned"], g - 1)
                    pool.wait_ge(q["w_ready"], g - 1)
                pool.tensor_copy(idx[s][:], r["tok_i"][:, bass.ds(g, 1)]).then_inc(q["idx_ready"], 1)
                pool.wait_ge(q["idx_ready"], g + 1)
                apart(pool, q["passed"])
                pool.indirect_dma_start(out=xg[s][:], out_offset=None, in_=rows,
                                        in_offset=bass.IndirectOffsetOnAxis(ap=idx[s][:, 0:1], axis=0)
                                        ).then_inc(xg_in[s], 16)

            for s in range(2):
                gather(s, s, True)
            with pool.Fori(1, NG // 2) as k:
                for s in range(2):
                    gather(2 * k + s, s, False)

        @block.tensor
        def _(pe):
            def turn(g, s, nth):
                pe.wait_ge(raw_in[s], 64 * nth)
                pe.wait_ge(q["sb_gu0"], g)
                pe.wait_ge(q["sb_gu1"], g)
                for k in range(DC):
                    for w, raw in enumerate((raw_g, raw_u)):
                        for h in range(2):
                            col = w * EG * F + h * P
                            pe.transpose(b_gu[k][:, col:col + P], raw[s][:, h, k * P:(k + 1) * P], c["ident"][:])
                pe.wait_ge(q["sb_d"], g)
                for h in range(2):
                    for k in range(DC):
                        pe.transpose(b_d[:, h * D + k * P:h * D + (k + 1) * P],
                                     raw_d[s][:, k, 2 * h:2 * h + 2, :].rearrange("p e f -> p (e f)"), c["ident"][:])
                pe.wait_ge(xg_in[s], 16 * nth)
                pe.wait_ge(q["sb_x"], g)
                for k in range(DC):
                    ins = pe.transpose(b_x[:, k * P:(k + 1) * P], xg[s][:, k * P:(k + 1) * P], c["ident"][:])
                ins.then_inc(q["turned"], 1)

            def outputs(n, s):
                pe.wait_ge(q["sb_h"], n + 1)
                pe.wait_ge(q["sb_d"], n + 1)
                pe.wait_ge(q["y_lo"], n)
                for h in range(2):
                    ins = pe.matmul(b_y[:, 0:D], hT[s][:, h, :], dT[s][:, h, :], start=(h == 0), stop=(h == 1))
                ins.then_inc(q["y_done"], 1)

            def expert(g, s, more, first=False):
                pe.wait_ge(q["sb_gu0"], g + 1)
                pe.wait_ge(q["sb_gu1"], g + 1)
                pe.wait_ge(q["sb_x"], g + 1)
                pe.wait_ge(q["hid_ready"], g)
                for k in range(DC):
                    ins = pe.matmul(b_act[:], xgT[s][:, k, :], guT[s][:, k, :], start=(k == 0), stop=(k == DC - 1))
                ins.then_inc(q["gu_done"], 1)
                if more is not None:
                    turn(g + 1, 1 - s, more)
                if not first:
                    outputs(g - 1, 1 - s)
                pe.wait_ge(q["hid_ready"], g + 1)
                pe.wait_ge(q["sb_h"], g)
                for h in range(2):
                    ins = pe.transpose(b_h[:, h * P:(h + 1) * P], hid[s][:, h * P:(h + 1) * P], c["ident"][:])
                ins.then_inc(q["h_turned"], 1)

            turn(0, 0, 1)
            expert(0, 0, 1, True)
            expert(1, 1, 2)
            with pe.Fori(1, NG // 2 - 1) as k:
                expert(2 * k, 0, k + 1)
                expert(2 * k + 1, 1, k + 2)
            expert(NG - 2, 0, NG // 2)
            expert(NG - 1, 1, None)
            outputs(NG - 1, 1)

            pe.wait_ge(q["y_lo"], NG)
            def collect(i, s, first):
                pe.wait_ge(q["hot_ready"], i + 1)
                if not first:
                    pe.wait_ge(q["x_done"], i - 1)
                for g in range(NG):
                    ins = pe.matmul(sums[s][:], hot[s][:, g, :], y[:, g, :, :].rearrange("p a b -> p (a b)"),
                                    start=(g == 0), stop=(g == NG - 1))
                ins.then_inc(q["sum_done"], 1)

            collect(0, 0, True)
            collect(1, 1, True)
            with pe.Fori(1, NT // 2) as k:
                for s in range(2):
                    collect(2 * k + s, s, False)

        @block.scalar
        def _(act):
            def turned(g, s):
                act.wait_ge(q["turned"], g + 1)
                if not isinstance(g, int) or g >= 2:
                    act.wait_ge(q["gu_done"], g - 1)
                act.activation(guT[s][:, 0, :], b_gu[0][:], ACT.Copy).then_inc(q["sb_gu0"], 1)
                act.activation(xgT[s][:], b_x[:, 0:D].rearrange("p (k t) -> p k t", k=DC),
                               ACT.Copy).then_inc(q["sb_x"], 1)

            def outputs(n, s):
                act.wait_ge(q["y_done"], n + 1)
                act.wait_ge(q["w_ready"], n + 1)
                act.activation(y[:, bass.ds(n, 1), 0, :], b_y[:, 0:D], ACT.Copy, scale=ws[s][:, 0:1]).then_inc(q["y_hi"], 1)

            def expert(g, s, more, first=False):
                act.wait_ge(q["gu_done"], g + 1)
                act.wait_ge(q["sb_gu1"], g + 1)
                for e in range(EG):
                    ps = slice(e * CAP, (e + 1) * CAP)
                    ins = act.activation(sil[s][ps, :], b_act[ps, e * F:(e + 1) * F], ACT.Silu)
                ins.then_inc(q["sil_done"], 1)
                if more:
                    turned(g + 1, 1 - s)
                if not first:
                    outputs(g - 1, 1 - s)
                act.wait_ge(q["h_turned"], g + 1)
                act.activation(hT[s][:], b_h[:, 0:2 * P].rearrange("p (h t) -> p h t", h=2),
                               ACT.Copy).then_inc(q["sb_h"], 1)

            turned(0, 0)
            expert(0, 0, True, True)
            expert(1, 1, True)
            with act.Fori(1, NG // 2 - 1) as k:
                for s in range(2):
                    expert(2 * k + s, s, True)
            expert(NG - 2, 0, True)
            expert(NG - 1, 1, False)
            outputs(NG - 1, 1)

        @block.vector
        def _(dve):
            def one_hot(i, s):
                dve.tensor_tensor(hot[s][:], c["iota_t"][:, bass.ds(i * P, P)].unsqueeze(1).broadcast_to([P, NG, P]),
                                  r["tok"][:].unsqueeze(2).broadcast_to([P, NG, P]), ALU.is_equal
                                  ).then_inc(q["hot_ready"], 1)

            for s in range(2):
                dve.memset(hid[s][:], 0.0).then_inc(q["zeroed"], 1)
            dve.wait_ge(q["zeroed"], 2)

            def outputs(n, s):
                dve.wait_ge(q["y_hi"], n + 1)
                dve.wait_ge(q["w_ready"], n + 1)
                dve.scalar_tensor_tensor(out=y[:, bass.ds(n, 1), 1, :], in0=b_y[:, 0:D], scalar=ws[s][:, 0:1],
                                         in1=f32(y[:, bass.ds(n, 1), 0, :]), op0=ALU.mult,
                                         op1=ALU.subtract).then_inc(q["y_lo"], 1)

            def turned(g, s, first):
                dve.wait_ge(q["turned"], g + 1)
                if not first:
                    dve.wait_ge(q["gu_done"], g - 1)
                dve.tensor_copy(guT[s][:, 1, :], b_gu[1][:]).then_inc(q["sb_gu1"], 1)
                if not first:
                    dve.wait_ge(q["y_done"], g - 1)
                dve.tensor_copy(dT[s][:].rearrange("p h d -> p (h d)"), b_d[:]).then_inc(q["sb_d"], 1)
                if not first:
                    outputs(g - 2, s)
                    dve.wait_ge(q["y_lo"], g - 1)
                dve.tensor_tensor(wtmp[s][:], xg[s][:, D:ROW], c["sel"][:, bass.ds(60 - EG * g, E)],
                                  ALU.mult).then_inc(q["w_step"], 1)
                dve.wait_ge(q["w_step"], g + 1)
                dve.tensor_reduce(ws[s][:], wtmp[s][:], X, ALU.add).then_inc(q["w_ready"], 1)

            def expert(g, s, more, first=False):
                dve.wait_ge(q["sil_done"], g + 1)
                if not first:
                    dve.wait_ge(q["h_turned"], g - 1)
                for e in range(EG):
                    ps = slice(e * CAP, (e + 1) * CAP)
                    ins = dve.tensor_tensor(hid[s][ps, e * F:(e + 1) * F],
                                            b_act[ps, EG * F + e * F:EG * F + (e + 1) * F], sil[s][ps, :], ALU.mult)
                ins.then_inc(q["hid_ready"], 1)
                if more:
                    turned(g + 1, 1 - s, isinstance(g, int) and g + 1 < 2)
                else:
                    outputs(g - 1, 1 - s)

            turned(0, 0, True)
            expert(0, 0, True, True)
            expert(1, 1, True, True)
            with dve.Fori(1, NG // 2 - 1) as k:
                for s in range(2):
                    expert(2 * k + s, s, True)
            expert(NG - 2, 0, True)
            expert(NG - 1, 1, False)
            one_hot(0, 0)
            outputs(NG - 1, 1)

            def add(i, s):
                dve.wait_ge(q["sum_done"], i + 1)
                xs = c["x"][:, bass.ds(i, 1), :].rearrange("p a b -> p (a b)")
                for h in range(2):
                    ins = dve.scalar_tensor_tensor(out=xs, in0=sums[s][:, h * D:(h + 1) * D], scalar=0.5, in1=xs,
                                                   op0=ALU.mult, op1=ALU.add)
                    if h == 0:
                        ins.then_inc(q["x_part"], 1)
                        dve.wait_ge(q["x_part"], i + 1)
                ins.then_inc(q["x_done"], 1)

            one_hot(1, 1)
            with dve.Fori(0, NT // 2 - 1) as k:
                for s in range(2):
                    add(2 * k + s, s)
                    one_hot(2 * k + s + 2, s)
            for s in range(2):
                add(NT - 2 + s, s)


def attention(nc, c, a, tag):
    with ExitStack() as ctx:
        m = Memory(nc, ctx, tag)
        U = H * B
        xT = [m.sb(f"xT{k}", [P, DC, N], F32R) for k in range(2)]
        nb, ns = norm_buffers(m), norm_sems(m)
        raw_c = m.sb("raw_c", [P, 4, D])
        raw_s = m.sb("raw_s", [P, 4, D])
        w = [[m.sb(f"w{k}_{s}", [P, 4, D], F32R) for k in range(2)] for s in range(2)]
        qT = [[m.sb(f"qT{k}_{s}", [P, S], F32R) for k in range(2)] for s in range(2)]
        kT = [[m.sb(f"kT{k}_{s}", [P, S], F32R) for k in range(2)] for s in range(2)]
        vT = m.sb("vT", [P, S])
        v = [[m.sb(f"v{k}_{s}", [P, 4, HD], F32R) for k in range(2)] for s in range(2)]
        pr = [m.sb(f"pr{s}", [P, 4, S]) for s in range(2)]
        prT = [[m.sb(f"prT{k}_{s}", [P, S], F32R) for k in range(2)] for s in range(2)]
        oT = [[m.sb(f"oT{k}_{s}", [P, S], F32R) for k in range(2)] for s in range(2)]
        junk = [m.sb(f"junk{s}", [P, S], BF16) for s in range(2)]
        nmax = m.sb("nmax", [P, 2, 4])
        rsum = m.sb("rsum", [P, 2, 4])
        rinv = m.sb("rinv", [P, 4, 4])
        b_s = [m.ps(f"b_s{s}") for s in range(2)]
        b_t = [m.ps(f"b_t{s}") for s in range(2)]
        b_o, b_out = m.ps("b_o"), m.ps("b_out")
        b_p = [m.ps(f"b_p{s}") for s in range(2)]
        nb["bank"] = b_s
        sems = ("raw_in w_mul w_hi w_ready bo_added s_done nmax_ready exp_done rinv_ready t_done pt_hi pt_lo pv_done "
                "q_done q_hi q_lo k_done k_hi k_lo vT_done vT_sb v_done v_hi v_lo o_done o_hi o_lo out_done x_added passed")
        q = {n: m.sem(n) for n in sems.split()}
        block = ctx.enter_context(nc.Block())
        LOADS = 11

        def late(t, n):
            return not isinstance(t, int) or t >= n

        def schedule(eng, step):
            for u in range(4):
                step(u, u)
            with eng.Fori(0, 7) as k:
                for j in range(4, 12):
                    step(8 * k + j, j)
            for u in range(60, U):
                step(u, u)

        def later(u, n):
            return not isinstance(u, int) or u + n < U

        @block.sync
        def _(sp):
            def load(h):
                for n, name in enumerate(("wq", "wk", "wv")):
                    sp.dma_start(raw_c[:, n, :].rearrange("p (c f) -> p c f", c=DC),
                                 a[name + "_codes"].rearrange("(c p) f -> p c f", p=P)[:, :, bass.ds(h * HD, HD)]
                                 ).then_inc(q["raw_in"], 16)
                    for k in range(DC):
                        rows = a[name + "_scales"][k * (P // BLK):(k + 1) * (P // BLK), bass.ds(h * HD, HD)]
                        sp.dma_start(raw_s[:, n, k * HD:(k + 1) * HD],
                                     rows.unsqueeze(1).broadcast_to([P // BLK, BLK, HD])).then_inc(q["raw_in"], 16)
                sp.dma_start(raw_c[:, 3, :], a["wo_codes"][bass.ds(h * HD, HD), :]).then_inc(q["raw_in"], 16)
                rows = a["wo_scales"][bass.ds(h * (HD // BLK), HD // BLK), :]
                sp.dma_start(raw_s[:, 3, :], rows.unsqueeze(1).broadcast_to([HD // BLK, BLK, D])).then_inc(q["raw_in"], 16)

            load(0)
            with sp.Fori(1, H) as h:
                sp.wait_ge(q["w_ready"], h)
                load(h)

        @block.gpsimd
        def _(pool):
            def weights(h, s):
                pool.wait_ge(q["raw_in"], 16 * LOADS * (h + 1))
                pool.tensor_tensor(raw_c[:], raw_c[:], raw_s[:], ALU.mult).then_inc(q["w_mul"], 1)
                pool.wait_ge(q["w_mul"], h + 1)
                if late(h, 2):
                    pool.wait_ge(q["out_done"], 2 * B * (h - 1))
                apart(pool, q["passed"])
                pool.tensor_copy(w[s][0][:], raw_c[:]).then_inc(q["w_hi"], 1)
                pool.wait_ge(q["w_hi"], h + 1)
                pool.tensor_tensor(w[s][1][:], raw_c[:], f32(w[s][0][:]), ALU.subtract).then_inc(q["w_ready"], 1)

            norm_pool(pool, c, nb, ns)
            weights(0, 0)
            pool.wait_ge(ns["xn_ready"], NT // 2)
            pool.tensor_tensor(c["x"][:], c["x"][:], c["bo"][:].unsqueeze(1).broadcast_to([P, NT, D]),
                               ALU.add).then_inc(q["bo_added"], 1)
            weights(1, 1)
            with pool.Fori(1, H // 2) as k:
                for s in range(2):
                    weights(2 * k + s, s)

        @block.tensor
        def _(pe):
            def mm3(out, lhs, rhs, first, last):
                pe.matmul(out, lhs[0], rhs[0], start=first, stop=False)
                pe.matmul(out, lhs[0], rhs[1], start=False, stop=False)
                return pe.matmul(out, lhs[1], rhs[0], start=False, stop=last)

            def project(bank, n, j):
                b0, s = (j % 4) * S, (j // 4) % 2
                for d in range(DC):
                    ins = mm3(bank[:], [t[:, n, d * HD:(d + 1) * HD] for t in w[s]], [t[:, d, b0:b0 + S] for t in xT],
                              d == 0, d == DC - 1)
                return ins

            def queries(u, j, hd):
                if j % 4 == 0:
                    pe.wait_ge(q["w_ready"], hd + 1)
                if late(u, 2):
                    pe.wait_ge(q["vT_sb"], u - 1)
                elif u == 1:
                    pe.wait_ge(q["q_lo"], 1)
                project(b_p[0], 0, j).then_inc(q["q_done"], 1)

            def keys(u, j):
                if late(u, 2):
                    pe.wait_ge(q["v_lo"], u - 1)
                elif u == 1:
                    pe.wait_ge(q["k_lo"], 1)
                project(b_p[1], 1, j).then_inc(q["k_done"], 1)

            def values(u, j):
                pe.wait_ge(q["q_lo"], u + 2 if later(u, 1) else U)
                project(b_p[0], 2, j).then_inc(q["vT_done"], 1)

            def turn_values(u):
                pe.wait_ge(q["k_lo"], u + 2 if later(u, 1) else U)
                pe.wait_ge(q["vT_sb"], u + 1)
                for t in range(4):
                    ins = pe.transpose(b_p[1][:, t * P:(t + 1) * P], vT[:, t * P:(t + 1) * P], c["ident"][:])
                ins.then_inc(q["v_done"], 1)

            def scores(u, j, i):
                if i == 0:
                    pe.wait_ge(q["q_lo"], u + 1)
                    pe.wait_ge(q["k_lo"], u + 1)
                if late(4 * u + i if isinstance(u, int) else u, 2):
                    pe.wait_ge(q["exp_done"], 4 * u + i - 1)
                mm3(b_s[i % 2][:], [t[:, i * P:(i + 1) * P] for t in qT[j % 2]], [t[:] for t in kT[j % 2]],
                    True, True).then_inc(q["s_done"], 1)

            def turn_probs(u, j, kb):
                if kb == 0:
                    pe.wait_ge(q["exp_done"], 4 * u + 4)
                if late(4 * u + kb if isinstance(u, int) else u, 2):
                    pe.wait_ge(q["pt_lo"], 4 * u + kb - 1)
                for i in range(4):
                    ins = pe.transpose(b_t[kb % 2][:, i * P:(i + 1) * P], pr[j % 2][:, i, kb * P:(kb + 1) * P],
                                       c["ident"][:])
                ins.then_inc(q["t_done"], 1)

            def probs_values(u, j, kb):
                pe.wait_ge(q["pt_lo"], 4 * u + kb + 1)
                if kb == 0:
                    pe.wait_ge(q["v_lo"], u + 1)
                    pe.wait_ge(q["o_lo"], u)
                ins = mm3(b_o[:], [t[:, kb, :] for t in v[j % 2]], [t[:] for t in prT[kb % 2]], kb == 0, kb == 3)
                ins.then_inc(q["pv_done"], 1)

            def output(u, j, o):
                if o == 0:
                    pe.wait_ge(q["o_lo"], u + 1)
                pe.wait_ge(q["x_added"], 2 * u + o)
                for t in range(2):
                    i = 2 * o + t
                    ins = mm3(b_out[:, t * D:(t + 1) * D], [z[:, i * P:(i + 1) * P] for z in oT[j % 2]],
                              [z[:, 3, :] for z in w[(j // 4) % 2]], True, True)
                ins.then_inc(q["out_done"], 1)

            def step(u, j):
                for i in range(4):
                    turn_probs(u, j, i)
                    if later(u, 1):
                        scores(u + 1, j + 1, i)
                    if i > 0:
                        probs_values(u, j, i - 1)
                    if i == 0 and late(u, 2):
                        output(u - 2, j + 6, 1)
                    if i == 0 and later(u, 2):
                        queries(u + 2, j + 2, (u - j) // 4 + (j + 2) // 4)
                    if i == 1 and later(u, 2):
                        keys(u + 2, j + 2)
                    if i == 2 and later(u, 1):
                        values(u + 1, j + 1)
                    if i == 2 and late(u, 1):
                        output(u - 1, j + 7, 0)
                    if i == 3 and later(u, 1):
                        turn_values(u + 1)
                probs_values(u, j, 3)

            norm_tensor(pe, c, nb, ns)
            pe.wait_ge(ns["lo_done"], NT // 2)
            for u in range(2):
                queries(u, u, 0)
                keys(u, u)
            values(0, 0)
            turn_values(0)
            for i in range(4):
                scores(0, 0, i)
            schedule(pe, step)
            output(U - 2, U - 2, 1)
            for o in range(2):
                output(U - 1, U - 1, o)

        @block.scalar
        def _(act):
            def queries(u, j):
                act.wait_ge(q["q_done"], u + 1)
                if late(u, 2):
                    act.wait_ge(q["s_done"], 4 * (u - 1))
                apart(act, q["passed"])
                act.activation(qT[j % 2][0][:], b_p[0][:], ACT.Identity, bias=bias(c["bq"], u, j)).then_inc(q["q_hi"], 1)

            def keys(u, j):
                act.wait_ge(q["k_done"], u + 1)
                apart(act, q["passed"])
                act.activation(kT[j % 2][0][:], b_p[1][:], ACT.Identity, bias=bias(c["bk"], u, j)).then_inc(q["k_hi"], 1)

            def bias(t, u, j):
                return t[:, bass.ds((u - j) // 4 + j // 4, 1)]

            def values(u, j):
                act.wait_ge(q["vT_done"], u + 1)
                act.wait_ge(q["v_done"], u)
                apart(act, q["passed"])
                act.activation(vT[:], b_p[0][:], ACT.Identity, bias=bias(c["bv"], u, j)).then_inc(q["vT_sb"], 1)

            def turned_values(u, j):
                act.wait_ge(q["v_done"], u + 1)
                if late(u, 1):
                    act.wait_ge(q["pv_done"], 4 * (u - 1))
                act.activation(v[j % 2][0][:].rearrange("p t d -> p (t d)"), b_p[1][:], ACT.Copy).then_inc(q["v_hi"], 1)

            def exps(u, j, i):
                if i == 0 and late(u, 1):
                    act.wait_ge(q["t_done"], 4 * (u - 1))
                    act.wait_ge(q["rinv_ready"], u - 1)
                act.wait_ge(q["nmax_ready"], 4 * u + i + 1)
                act.activation(pr[j % 2][:, i, :], b_s[i % 2][:], ACT.Exp, bias=nmax[:, j % 2, i:i + 1], scale=SCALE,
                               accum_out=rsum[:, j % 2, i:i + 1]).then_inc(q["exp_done"], 1)

            def turned_probs(u, kb):
                act.wait_ge(q["t_done"], 4 * u + kb + 1)
                if late(4 * u + kb if isinstance(u, int) else u, 2):
                    act.wait_ge(q["pv_done"], 4 * u + kb - 1)
                act.activation(prT[kb % 2][0][:], b_t[kb % 2][:], ACT.Copy).then_inc(q["pt_hi"], 1)

            def outputs(u, j):
                act.wait_ge(q["pv_done"], 4 * u + 4)
                if late(u, 2):
                    act.wait_ge(q["out_done"], 2 * (u - 1))
                act.activation(oT[j % 2][0][:], b_o[:], ACT.Copy).then_inc(q["o_hi"], 1)

            def step(u, j):
                if late(u, 1):
                    outputs(u - 1, j + 7)
                for i in range(4):
                    turned_probs(u, i)
                    if i == 0 and late(u, 1):
                        turned_values(u, j)
                    if i == 1 and later(u, 2):
                        queries(u + 2, j + 2)
                    if i == 2 and later(u, 2):
                        keys(u + 2, j + 2)
                    if i == 3 and later(u, 1):
                        values(u + 1, j + 1)
                    if later(u, 1):
                        exps(u + 1, j + 1, i)

            norm_scalar(act, nb, ns, xT)
            for u in range(2):
                queries(u, u)
                keys(u, u)
            values(0, 0)
            turned_values(0, 0)
            for i in range(4):
                exps(0, 0, i)
            schedule(act, step)
            outputs(U - 1, U - 1)

        @block.vector
        def _(dve):
            def low(hi, bank, dst, ready, n, done):
                dve.wait_ge(q[ready], n)
                dve.tensor_tensor(dst, bank, f32(hi), ALU.subtract).then_inc(q[done], 1)

            def low_biased(t, bank, name, b, u, j):
                dve.wait_ge(q[name + "_hi"], u + 1)
                dve.scalar_tensor_tensor(out=t[j % 2][1][:], in0=bank[:], scalar=c[b][:, bass.ds((u - j) // 4 + j // 4, 1)],
                                         in1=f32(t[j % 2][0][:]), op0=ALU.add, op1=ALU.subtract
                                         ).then_inc(q[name + "_lo"], 1)

            def turned_values(u, j):
                hi, lo = (t[:].rearrange("p t d -> p (t d)") for t in v[j % 2])
                low(hi, b_p[1][:], lo, "v_hi", u + 1, "v_lo")

            def maxima(u, j, i):
                dve.wait_ge(q["s_done"], 4 * u + i + 1)
                dve.tensor_scalar(junk[i % 2][:], b_s[i % 2][:], -SCALE, None, ALU.mult, ALU.min,
                                  accum_out=nmax[:, j % 2, i:i + 1]).then_inc(q["nmax_ready"], 1)

            def add(u, j, o):
                dve.wait_ge(q["out_done"], 2 * u + o + 1)
                for t in range(2):
                    i = 2 * o + t
                    xs = c["x"][:, (j % 4) * 4 + i, :]
                    ins = dve.scalar_tensor_tensor(out=xs, in0=b_out[:, t * D:(t + 1) * D],
                                                   scalar=rinv[:, j % 4, i:i + 1], in1=xs, op0=ALU.mult, op1=ALU.add)
                ins.then_inc(q["x_added"], 1)

            def outputs(n, j):
                low(oT[j % 2][0][:], b_o[:], oT[j % 2][1][:], "o_hi", n, "o_lo")

            def step(u, j):
                if late(u, 1):
                    outputs(u, j + 7)
                for i in range(4):
                    low(prT[i % 2][0][:], b_t[i % 2][:], prT[i % 2][1][:], "pt_hi", 4 * u + i + 1, "pt_lo")
                    if later(u, 1):
                        maxima(u + 1, j + 1, i)
                    if i == 0:
                        if late(u, 4):
                            dve.wait_ge(q["x_added"], 2 * (u - 3))
                        dve.reciprocal(rinv[:, j % 4, :], rsum[:, j % 2, :]).then_inc(q["rinv_ready"], 1)
                        if late(u, 1):
                            turned_values(u, j)
                        else:
                            dve.wait_ge(q["bo_added"], 1)
                    if i == 1:
                        if later(u, 2):
                            low_biased(qT, b_p[0], "q", "bq", u + 2, j + 2)
                        if late(u, 2):
                            add(u - 2, j + 6, 1)
                    if i == 2 and later(u, 2):
                        low_biased(kT, b_p[1], "k", "bk", u + 2, j + 2)
                    if i == 3 and late(u, 1):
                        add(u - 1, j + 7, 0)

            norm_vector(dve, c, nb, ns, xT, False)
            for u in range(2):
                low_biased(qT, b_p[0], "q", "bq", u, u)
                low_biased(kT, b_p[1], "k", "bk", u, u)
            turned_values(0, 0)
            for i in range(4):
                maxima(0, 0, i)
            schedule(dve, step)
            outputs(U, U - 1)
            add(U - 2, U - 2, 1)
            for o in range(2):
                add(U - 1, U - 1, o)


def macaron_layer(nc, a, out):
    rows = nc.dram_tensor("rows", (N, ROW), F32).ap()
    tok_dram = nc.dram_tensor("tok_dram", (E, CAP), F32).ap()
    with ExitStack() as ctx:
        m = Memory(nc, ctx, "keep")
        c = prepare(nc, m, a)
        r = dict(tok=m.sb("tok", [P, NG]), tok_i=m.sb("tok_i", [P, NG], I32))
        ffn_shared_and_route(nc, c, r, rows, tok_dram, "f1")
        ffn_experts(nc, c, r, rows, a, None, "e1")
        attention(nc, c, a, "at")
        ffn_shared_and_route(nc, c, r, rows, tok_dram, "f2")
        ffn_experts(nc, c, r, rows, a, out.rearrange("b (i p) d -> (b i) p d", p=P), "e2")


NAMES = [("x", "L0_attn_x")] + [(f"{w}_{t}", f"L0_attn_{w}_{t}") for w in ("wq", "wk", "wv", "wo") for t in ("codes", "scales")] \
    + [(b, f"L0_attn_{b}") for b in ("bq", "bk", "bv", "bo")] \
    + [(f, f"L0_ffn_{f}") for f in ("router_w", "router_bias", "gate_w", "up_w", "down_w", "sh_gate_w", "sh_up_w",
                                    "sh_down_w")]


def kernel(**inputs):
    import concourse.bacc as bacc
    from concourse.bass_utils import run_bass_kernel_spmd

    nc = bacc.Bacc("TRN2", target_bir_lowering=False, num_devices=1)
    arrays, args = {}, {}
    for short, name in NAMES:
        arr = np.ascontiguousarray(inputs[name])
        arrays[f"in_{short}"] = arr
        args[short] = nc.dram_tensor(f"in_{short}", arr.shape, mybir.dt.from_np(arr.dtype), kind="ExternalInput").ap()
    out = nc.dram_tensor("out", (B, S, D), F32, kind="ExternalOutput").ap()
    macaron_layer(nc, args, out)
    result = run_bass_kernel_spmd(nc, [arrays], core_ids=[0])
    return result.results[0]["out"]
```
